# Optimizing a Trainium2 kernel written in Bass

```python
import numpy as np
import jax
import jax.numpy as jnp

def _softmax(x, axis=-1):
    return jax.nn.softmax(x, axis=axis)

def _gelu(x):
    return jax.nn.gelu(x, approximate=True)

def _silu(x):
    return jax.nn.silu(x)

def _sigmoid(x):
    return jax.nn.sigmoid(x)

def _layernorm(x, axis=-1, eps=1e-05):
    m = jnp.mean(x, axis=axis, keepdims=True)
    v = jnp.var(x, axis=axis, keepdims=True)
    return (x - m) / jnp.sqrt(v + eps)

def _scatter_add(tgt, idx, src, axis=0):
    return tgt.at[idx].add(src)

def _segment_sum(src, seg, n):
    return jax.ops.segment_sum(src, seg, n)
kernel_name = 'mk_vit_tower_cls_d1_tok_img1024_r4_2dd9b1'

def setup_inputs(seed: int=0):
    np.random.seed(seed)
    _w = jnp.asarray

    def _rec_inputs():
        import jax
        import jax.numpy as jnp
        _rk = jax.random.key(seed)
        x = jax.random.uniform(jax.random.fold_in(_rk, 1), (16, 3, 256, 256), jnp.float32, 0.0, 1)
        cls_tok = 0.02 * jax.random.normal(jax.random.fold_in(_rk, 5), (1, 1, 256), jnp.float32)
        return (x, cls_tok)
    x, cls_tok = _rec_inputs()

    def _L0_tok_setup():
        import jax, jax.numpy as jnp
        import numpy as np
        _GRAY_W = (0.2989, 0.587, 0.114)
        key = jax.random.key(seed)
        x = jax.random.uniform(key, (32, 3, 256, 256), dtype=jnp.float32)
        sx = jnp.array([[-3.0, 0.0, 3.0], [-10.0, 0.0, 10.0], [-3.0, 0.0, 3.0]], dtype=jnp.float32)
        scharr = jnp.stack([sx, sx.T])[:, None, :, :]
        return {'x': x, 'scharr': scharr}
    _L0_tok_all = _L0_tok_setup()
    _L0_tok_in = {k: v for k, v in _L0_tok_all.items() if k in ('scharr',)}
    del _L0_tok_all

    def _L0_attn_setup():
        import jax, jax.numpy as jnp
        import numpy as np
        D_MODEL = 256
        NHEAD = 16
        D_K = D_MODEL // NHEAD
        WINDOW = 128
        NEG_INF = -1e+30
        key = jax.random.key(seed)
        k1, k2, k3 = jax.random.split(key, 3)
        B, T = (2, 512)
        x = jax.random.normal(k1, (B, T, D_MODEL), dtype=jnp.float32)
        W_qkv = jax.random.normal(k2, (D_MODEL, 3 * D_MODEL), dtype=jnp.float32) * D_MODEL ** (-0.5)
        W_out = jax.random.normal(k3, (D_MODEL, D_MODEL), dtype=jnp.float32) * D_MODEL ** (-0.5)
        return {'x': x, 'W_qkv': W_qkv, 'W_out': W_out}
    _L0_attn_all = _L0_attn_setup()
    _L0_attn_in = {k: v for k, v in _L0_attn_all.items() if k in ('W_qkv', 'W_out')}
    del _L0_attn_all

    def _L0_ffn_setup():
        import jax, jax.numpy as jnp
        import numpy as np
        HID = 256
        NH = 16
        NKV = 4
        HD = HID // NH
        E = 8
        TOPK = 2
        FFN = 512
        EPS = 1e-05
        THETA = 10000.0

        def _rmsnorm(x, w):
            var = jnp.mean(x * x, axis=-1, keepdims=True)
            return x * jax.lax.rsqrt(var + EPS) * w

        def _rope_tables(S):
            inv_freq = 1.0 / THETA ** (jnp.arange(0, HD, 2, dtype=jnp.float32) / HD)
            freqs = jnp.arange(S, dtype=jnp.float32)[:, None] * inv_freq[None, :]
            emb = jnp.concatenate([freqs, freqs], axis=-1)
            return (jnp.cos(emb), jnp.sin(emb))

        def _apply_rope(t, cos, sin):
            t1, t2 = jnp.split(t, 2, axis=-1)
            rot = jnp.concatenate([-t2, t1], axis=-1)
            return t * cos[None, :, None, :] + rot * sin[None, :, None, :]
        key = jax.random.key(seed)
        ks = jax.random.split(key, 6)
        B, S = (1, 512)
        x = jax.random.normal(ks[0], (B, S, HID), dtype=jnp.float32)
        wqkv = jax.random.normal(ks[1], ((NH + 2 * NKV) * HD, HID), dtype=jnp.float32) * 0.02
        wo = jax.random.normal(ks[2], (HID, NH * HD), dtype=jnp.float32) * 0.02
        gate_w = jax.random.normal(ks[3], (E, HID), dtype=jnp.float32) * 0.02
        w13 = jax.random.normal(ks[4], (E, 2 * FFN, HID), dtype=jnp.float32) * 0.02
        w2 = jax.random.normal(ks[5], (E, HID, FFN), dtype=jnp.float32) * 0.02
        return {'x': x, 'ln1_w': jnp.ones((HID,), jnp.float32), 'ln2_w': jnp.ones((HID,), jnp.float32), 'wqkv': wqkv, 'wo': wo, 'gate_w': gate_w, 'w13': w13, 'w2': w2}
    _L0_ffn_all = _L0_ffn_setup()
    _L0_ffn_in = {k: v for k, v in _L0_ffn_all.items() if k in ('ln1_w', 'ln2_w', 'wqkv', 'wo', 'gate_w', 'w13', 'w2')}
    del _L0_ffn_all
    return {'x': x, 'cls_tok': cls_tok, 'L0_tok_scharr': _L0_tok_in['scharr'], 'L0_attn_W_qkv': _L0_attn_in['W_qkv'], 'L0_attn_W_out': _L0_attn_in['W_out'], 'L0_ffn_ln1_w': _L0_ffn_in['ln1_w'], 'L0_ffn_ln2_w': _L0_ffn_in['ln2_w'], 'L0_ffn_wqkv': _L0_ffn_in['wqkv'], 'L0_ffn_wo': _L0_ffn_in['wo'], 'L0_ffn_gate_w': _L0_ffn_in['gate_w'], 'L0_ffn_w13': _L0_ffn_in['w13'], 'L0_ffn_w2': _L0_ffn_in['w2']}

def reference(x, cls_tok, L0_tok_scharr, L0_attn_W_qkv, L0_attn_W_out, L0_ffn_ln1_w, L0_ffn_ln2_w, L0_ffn_wqkv, L0_ffn_wo, L0_ffn_gate_w, L0_ffn_w13, L0_ffn_w2):
    import jax
    import jax.numpy as jnp

    def _L0_tok_ref(x, scharr):
        import jax, jax.numpy as jnp
        import numpy as np
        _GRAY_W = (0.2989, 0.587, 0.114)
        w = jnp.asarray(_GRAY_W, dtype=x.dtype)
        gray = jnp.einsum('bchw,c->bhw', x, w)[:, None]
        edges = jax.lax.conv_general_dilated(gray, scharr, window_strides=(1, 1), padding='SAME', dimension_numbers=('NCHW', 'OIHW', 'NCHW'))
        abs_edges = jnp.sqrt(jnp.square(edges))
        edge = abs_edges.sum(axis=1) / 2
        return edge

    def _L0_attn_ref(x, W_qkv, W_out):
        import jax, jax.numpy as jnp
        import numpy as np
        D_MODEL = 256
        NHEAD = 16
        D_K = D_MODEL // NHEAD
        WINDOW = 128
        NEG_INF = -1e+30
        B, T, D = x.shape
        H, dk = (NHEAD, D_K)
        qkv = (x @ W_qkv).reshape(B, T, 3, H, dk).transpose(2, 0, 3, 1, 4)
        Q, K, V = (qkv[0], qkv[1], qkv[2])
        scores = jnp.einsum('bhqd,bhkd->bhqk', Q, K) / jnp.sqrt(jnp.float32(dk))
        i = jnp.arange(T)[:, None]
        j = jnp.arange(T)[None, :]
        allowed = (j <= i) & (i - j < WINDOW)
        scores = jnp.where(allowed[None, None], scores, NEG_INF)
        attn = jax.nn.softmax(scores, axis=-1)
        out = jnp.einsum('bhqk,bhkd->bhqd', attn, V)
        out = out.transpose(0, 2, 1, 3).reshape(B, T, D)
        return out @ W_out

    def _L0_ffn_ref(x, ln1_w, ln2_w, wqkv, wo, gate_w, w13, w2):
        import jax, jax.numpy as jnp
        import numpy as np
        HID = 256
        NH = 16
        NKV = 4
        HD = HID // NH
        E = 8
        TOPK = 2
        FFN = 512
        EPS = 1e-05
        THETA = 10000.0

        def _rmsnorm(x, w):
            var = jnp.mean(x * x, axis=-1, keepdims=True)
            return x * jax.lax.rsqrt(var + EPS) * w

        def _rope_tables(S):
            inv_freq = 1.0 / THETA ** (jnp.arange(0, HD, 2, dtype=jnp.float32) / HD)
            freqs = jnp.arange(S, dtype=jnp.float32)[:, None] * inv_freq[None, :]
            emb = jnp.concatenate([freqs, freqs], axis=-1)
            return (jnp.cos(emb), jnp.sin(emb))

        def _apply_rope(t, cos, sin):
            t1, t2 = jnp.split(t, 2, axis=-1)
            rot = jnp.concatenate([-t2, t1], axis=-1)
            return t * cos[None, :, None, :] + rot * sin[None, :, None, :]
        B, S, _ = x.shape
        h = _rmsnorm(x, ln1_w)
        qkv = jnp.einsum('bsh,oh->bso', h, wqkv)
        q = qkv[..., :NH * HD].reshape(B, S, NH, HD)
        k = qkv[..., NH * HD:(NH + NKV) * HD].reshape(B, S, NKV, HD)
        v = qkv[..., (NH + NKV) * HD:].reshape(B, S, NKV, HD)
        cos, sin = _rope_tables(S)
        q = _apply_rope(q, cos, sin)
        k = _apply_rope(k, cos, sin)
        groups = NH // NKV
        k = jnp.repeat(k, groups, axis=2)
        v = jnp.repeat(v, groups, axis=2)
        scale = HD ** (-0.5)
        scores = jnp.einsum('bqhd,bkhd->bhqk', q, k) * scale
        causal = jnp.tril(jnp.ones((S, S), dtype=bool))
        scores = jnp.where(causal[None, None], scores, jnp.finfo(scores.dtype).min)
        probs = jax.nn.softmax(scores, axis=-1)
        attn = jnp.einsum('bhqk,bkhd->bqhd', probs, v).reshape(B, S, NH * HD)
        x = x + jnp.einsum('bso,ho->bsh', attn, wo)
        h = _rmsnorm(x, ln2_w).reshape(-1, HID)
        T = h.shape[0]
        logits = jnp.einsum('th,eh->te', h, gate_w)
        rprobs = jax.nn.softmax(logits.astype(jnp.float32), axis=-1)
        topw, topi = jax.lax.top_k(rprobs, TOPK)
        topw = topw / jnp.sum(topw, axis=-1, keepdims=True)
        wfull = jnp.zeros((T, E), jnp.float32).at[jnp.arange(T)[:, None], topi].set(topw)
        wfull = wfull.astype(h.dtype)
        out = jnp.zeros((T, HID), h.dtype)
        for e in range(E):
            w1 = w13[e, :FFN]
            w3 = w13[e, FFN:]
            g = jax.nn.silu(h @ w1.T) * (h @ w3.T)
            out = out + jnp.einsum('tf,hf->th', g, w2[e]) * wfull[:, e:e + 1]
        return x + out.reshape(B, S, HID)
    h = _L0_tok_ref(x, L0_tok_scharr)
    h = jnp.concatenate([jnp.broadcast_to(cls_tok, (h.shape[0], 1, h.shape[2])), h], axis=1)
    h = h + _L0_attn_ref(_layernorm(h, axis=-1), L0_attn_W_qkv, L0_attn_W_out)
    h = h + _L0_ffn_ref(_layernorm(h, axis=-1), L0_ffn_ln1_w, L0_ffn_ln2_w, L0_ffn_wqkv, L0_ffn_wo, L0_ffn_gate_w, L0_ffn_w13, L0_ffn_w2)
    return h

_drawn_inputs = setup_inputs


def setup_inputs(seed=0):
    import zlib

    import numpy as np

    out = dict(_drawn_inputs(seed))
    spreads = {'L0_ffn_ln1_w': (1.0, 0.6), 'L0_ffn_ln2_w': (1.0, 0.6)}
    factors = {'L0_ffn_wqkv': 5.837,
     'L0_ffn_wo': 6.478,
     'L0_ffn_gate_w': 8.0,
     'L0_ffn_w13': 8.0,
     'L0_ffn_w2': 8.0}
    for name, (base, spread) in spreads.items():
        noise = np.random.default_rng([zlib.crc32(name.encode()), seed]).standard_normal(out[name].shape)
        drawn = base * np.exp(spread * noise) if base else spread * noise
        out[name] = jnp.asarray(drawn.astype(out[name].dtype))
    for name, factor in factors.items():
        out[name] = (out[name] * factor).astype(out[name].dtype)
    return out
```

```python
from contextlib import ExitStack

import numpy as np

import concourse.bass as bass
from concourse import mybir

P = 128
ALU = mybir.AluOpType
ACT = mybir.ActivationFunctionType
AX = mybir.AxisListType
F32 = mybir.dt.float32
F32R = mybir.dt.float32r
BF16 = mybir.dt.bfloat16
I32 = mybir.dt.int32
U32 = mybir.dt.uint32

B, C3, HW = 16, 3, 256
D = 256
NT = HW // P
KT = D // P
NH, HD = 16, 16
NKV = 4
NE, FFN = 8, 512
FT = FFN // P
GRAY = (0.2989, 0.587, 0.114)
EPS = 1e-5
PAIRS = NH // 2
QC = P + 2
SC = QC + 2 * P + 2
KC = 2 * P + 2
TC = 3 * P
TOKENS = B * HW + 1
REGION = -(-(TOKENS + 2 * P) // P) * P
SLOTS = 2 * TOKENS
MT = -(-(SLOTS + NE * (P - 1)) // P)
MT += MT % 2
DUMP = NE * REGION
ITERS = B // 2
KV_HEADS = (NH, NKV)
K_TILES = (2, 1)
OWN_STEPS = 27
RT = B * NT + 1


def constants():
    k = np.arange(P)[:, None]
    m = np.arange(P)[None, :]
    shifts = np.stack([(k == m + dy - 1) for dy in range(3)], 1).astype(np.float32)
    ident = np.eye(P, dtype=np.float32)
    neg = np.float32(-1e30)
    q0, q1 = k, k + P
    s0, s1 = m, m + P
    cls = np.ones((P, 2), bool)

    def grow(ok):
        return np.where(ok, np.float32(0), neg)

    win = [lambda q, s: (s <= q) & (q - s < 128), lambda q, s: s <= q]
    ms, mt = [], []
    for a in range(2):
        see = win[a]
        c0 = cls & ((q0 + 1 < 128) if a == 0 else True)
        c1 = cls & (a == 1)
        ms.append(grow(np.concatenate([c0, see(q0, s0), c1, see(q1, s0), see(q1, s1)], 1)))
        mt.append(grow(np.concatenate([see(m, k), see(m + P, k), see(m + P, k + P)], 1)))
    mask_s = np.stack(ms, 1)
    mask_t = np.stack(mt, 1)
    inv = (np.float32(1.0) / np.float32(10000.0) ** (np.arange(0, HD, 2, dtype=np.float32) / np.float32(HD)))
    pos = (np.arange(NT, dtype=np.float32)[None, :] * P + np.arange(P, dtype=np.float32)[:, None] + 1)
    ang = (pos[:, :, None] * inv[None, None, :]).astype(np.float32)
    rope = np.stack([np.cos(ang), np.sin(ang)], 1).astype(np.float32)
    prefix = np.concatenate([(k < m), np.ones((P, P))], 1).astype(np.float32)
    small = np.zeros((P, 256), np.float32)
    small[:, 0:8] = np.arange(8)
    small[:, 8:41] = np.arange(33) * P
    small[:, 41] = np.arange(P)
    small[:, 42] = np.arange(P) == 0
    small[:, 43:45] = np.where(np.arange(P)[:, None] == 0, 0, DUMP + np.arange(P)[:, None] + P * np.arange(2))
    small[:, 45:53] = np.arange(8) * REGION
    small[:, 53:55] = -0.5
    small[:, 64:64 + MT] = np.arange(MT)
    return {"c_shift": shifts, "c_ident": ident, "c_masks": mask_s, "c_maskt": mask_t,
            "c_rope": rope, "c_prefix": prefix, "c_small": small}


def vit_tower(nc, x, cls_tok, scharr, wqkv1, wout1, ln1, ln2, wqkv2, wo2, gate, w13, w2,
              c_shift, c_ident, c_masks, c_maskt, c_rope, c_prefix, c_small, out):
    hs = nc.dram_tensor("hs", [DUMP + 2 * P, D], F32, kind="Internal").ap()
    ys = nc.dram_tensor("ys", [MT * P, D], F32, kind="Internal").ap()
    rs = nc.dram_tensor("rs", [B, P, NT * D], F32, kind="Internal").ap()

    qd = [nc.dram_tensor(f"qd{s}", [2, 2, P, 2 * P], F32, kind="Internal").ap() for s in range(2)]
    kd = [nc.dram_tensor(f"kd{s}", [2, 2, P, 2 * P], F32, kind="Internal").ap() for s in range(2)]
    md = [nc.dram_tensor(f"md{s}", [2 * NH, 2 * P], F32, kind="Internal").ap() for s in range(2)]

    sems = {}
    root = ExitStack()

    def sem(name):
        if name not in sems:
            sems[name] = root.enter_context(nc.semaphore(name))
        return sems[name]

    def sb(ctx, name, shape, dt=F32):
        return ctx.enter_context(nc.sbuf_tensor(name, shape, dt))

    with root:
        small = sb(root, "small", [P, 256])
        ident = sb(root, "ident", [P, P])
        idle = sb(root, "idle", [P, 4])
        route = sb(root, "route", [P, RT, 6])
        counts = sb(root, "counts", [P, NE])
        cls_res = sb(root, "cls_res", [P, D])
        bank = [root.enter_context(nc.psum_tensor(f"bank{n}", [P, 512], F32)) for n in range(8)]

        A = ExitStack()
        shift = sb(A, "shift", [P, 3, P])
        prefix = sb(A, "prefix", [P, 2, P], BF16)
        identb = sb(A, "identb", [P, P], BF16)
        mask_s = sb(A, "mask_s", [P, 2, SC], BF16)
        mask_t = sb(A, "mask_t", [P, 2, TC], BF16)
        rope = sb(A, "rope", [P, 2, NT, 8])
        taps = sb(A, "taps", [P, 2, 3, 3])
        band = sb(A, "band", [P, 2, 3, P])
        edgew = sb(A, "edgew", [6, 2, P])
        lnw = sb(A, "lnw", [P, 2, KT])
        w_qkv1 = sb(A, "w_qkv1", [P, KT, 3 * D])
        w_out1 = sb(A, "w_out1", [P, KT, D])
        w_qkv2 = sb(A, "w_qkv2", [P, KT, 384])
        w_out2 = sb(A, "w_out2", [P, KT, D])
        w_gate = sb(A, "w_gate", [P, KT, NE])
        vc = [sb(A, f"vc{a}", [P, NH, HD + 1]) for a in range(2)]
        prob = [sb(A, f"prob{n}", [P, 2, TC]) for n in range(2)]
        stage = sb(A, "stage", [P, 1024])

        class Slot:
            pass

        slots = []
        for s in range(2):
            z = Slot()
            slots.append(z)
            z.s = s
            z.xin = sb(A, f"xin{s}", [P, NT, C3, HW])
            z.gray = sb(A, f"gray{s}", [P, NT, HW + 2])
            z.halo = sb(A, f"halo{s}", [6, NT, HW])
            z.h0 = sb(A, f"h0{s}", [P, NT, D])
            z.tmp = sb(A, f"tmp{s}", [P, NT, D])
            z.y = sb(A, f"y{s}", [P, NT, D])
            z.hn = sb(A, f"hn{s}", [P, NT, D])
            z.yT = sb(A, f"yT{s}", [P, KT, 2 * P])
            z.xn = sb(A, f"xn{s}", [P, NT, D])
            z.res = sb(A, f"res{s}", [P, NT, D])
            z.qhl = sb(A, f"qhl{s}", [P, 2, 2, 2 * P], F32R)
            z.khl = sb(A, f"khl{s}", [P, 2, 2, 2 * P], F32R)
            z.v = [sb(A, f"v1{s}", [P, NT, NH, HD + 1]), sb(A, f"v2{s}", [P, NT, NKV, HD + 1])]
            z.qkv = sb(A, f"qkv{s}", [P, NT, 24, HD])
            z.rot = sb(A, f"rot{s}", [P, NT, 20, HD])
            z.ra = sb(A, f"ra{s}", [P, 4, NT * 20 * 8])
            z.osum = sb(A, f"osum{s}", [P, NT, NH, HD + 1])
            z.ocls = sb(A, f"ocls{s}", [P, NT, NH, HD + 1])
            z.rden = sb(A, f"rden{s}", [P, NT, NH])
            z.mx = sb(A, f"mx{s}", [P, NT, NH])
            z.scls = sb(A, f"scls{s}", [P, NT, NH])
            z.pcls = sb(A, f"pcls{s}", [P, NT, NH])
            z.nm = sb(A, f"nm{s}", [P, NT, 2, NH], F32R)
            z.mT = sb(A, f"mT{s}", [32, 2 * P])
            z.bn = sb(A, f"bn{s}", [P, NT, 6])
            z.st = sb(A, f"st{s}", [P, NT, 2])
            z.va = sb(A, f"va{s}", [P, NT])
            z.vb = sb(A, f"vb{s}", [P, NT])
            z.rstd = sb(A, f"rstd{s}", [P, NT])
            z.rr = sb(A, f"rr{s}", [P, NT])
            z.lg = sb(A, f"lg{s}", [P, NT, NE])
            z.top = sb(A, f"top{s}", [P, NT, 8])
            z.idx = sb(A, f"idx{s}", [P, NT, 8], U32)
            z.oh = sb(A, f"oh{s}", [P, NT, 2, NE])
            z.pick = sb(A, f"pick{s}", [P, NT, NE], BF16)
            z.rk = sb(A, f"rk{s}", [P, NT, NE])
            z.rsel = sb(A, f"rsel{s}", [P, NT, 2, NE])
            z.ro = sb(A, f"ro{s}", [P, NT, 6])
            z.ew = sb(A, f"ew{s}", [P, NT, 2])
            z.posf = sb(A, f"posf{s}", [P, NT, 2])
            z.pos = sb(A, f"pos{s}", [P, NT, 2], I32)
        qst = sb(A, "qst", [66, NH, 2 * P], F32R)
        kst = [sb(A, "kst0", [66, NH, KC], F32R), sb(A, "kst1", [66, NKV, KC], F32R)]
        A.close()

        M = ExitStack()
        w13s = sb(M, "w13s", [P, KT, NE, 2 * FFN])
        w2s = sb(M, "w2s", [P, FT, NE, D])
        lnm = sb(M, "lnm", [P, KT])
        nt = sb(M, "nt", [P, NE])
        gt = sb(M, "gt", [P, NE, 33])
        start = sb(M, "start", [P, NE])
        over = sb(M, "over", [P, NE, MT])
        tile_e = sb(M, "tile_e", [P, MT])
        tile_s = sb(M, "tile_s", [P, MT])
        tile_l = sb(M, "tile_l", [P, MT])
        cap = sb(M, "cap", [P, MT])
        tile_i = sb(M, "tile_i", [P, 2, MT], I32)
        zrow = sb(M, "zrow", [P, D])
        zposf = sb(M, "zposf", [P, 2, NE])
        zpos = sb(M, "zpos", [P, 2, NE], I32)
        eqs = sb(M, "eqs", [P, RT * 2, NE])
        yposf = sb(M, "yposf", [P, RT, 2])
        ypos = sb(M, "ypos", [P, RT, 2], I32)
        xt = [sb(M, f"xt{n}", [P, D]) for n in range(2)]
        xT = [sb(M, f"xT{n}", [P, KT, P]) for n in range(2)]
        sg = [sb(M, f"sg{n}", [P, FFN]) for n in range(2)]
        gu = [sb(M, f"gu{n}", [P, FFN]) for n in range(2)]
        guT = [sb(M, f"guT{n}", [P, FT, P]) for n in range(2)]
        yo = [sb(M, f"yo{n}", [P, D]) for n in range(2)]
        fr = [sb(M, f"fr{n}", [P, NT, D]) for n in range(2)]
        fy = [sb(M, f"fy{n}", [P, NT, 2, D]) for n in range(2)]
        fw = [sb(M, f"fw{n}", [P, NT, 2]) for n in range(2)]
        fidx = [sb(M, f"fidx{n}", [P, NT, 2], I32) for n in range(2)]
        fo = [sb(M, f"fo{n}", [P, NT, D]) for n in range(2)]
        M.close()

        block = root.enter_context(nc.Block())

        G_STAGES = ["conv0", "conv1", "tr_y1", "q1", "k1", "v1", "mt1", "tr_o1", "out1",
                    "tr_y2", "qkv2a", "qkv2b", "tr_q2", "tr_k2", "mt2", "tr_o2", "out2",
                    "tr_x", "lgt", "rank"]
        G_USES = [(s, g) for s in range(2) for g in G_STAGES]
        assert len(G_USES) % 2 == 0

        def gbank(s, g):
            return bank[6 + G_USES.index((s, g)) % 2]

        def wait_apart(eng, which, value, col):
            eng.wait_ge(which, value)
            if eng is pool_engine[0]:
                return eng.tensor_tensor(idle[:, col:col + 1], small[:, 0:1], small[:, 0:1], ALU.add)
            else:
                return eng.memset(idle[:, col:col + 1], 0.0)

        pool_engine = []

        def written(i, s, g):
            return sem("g_written"), i * len(G_USES) + G_USES.index((s, g)) + 1

        def read_sem(s, g):
            return sem(f"bank{6 + G_USES.index((s, g)) % 2}_read")

        def read(i, s, g):
            return read_sem(s, g), i * (len(G_USES) // 2) + G_USES.index((s, g)) // 2 + 1

        def g_free(pe, i, s, g):
            pe.wait_ge(read_sem(s, g), i * (len(G_USES) // 2) + G_USES.index((s, g)) // 2)

        CLS = ["load", "shift_ok", "bn", "aggr", "var", "pow", "ln", "tr", "trc", "qkv", "kh", "kl", "vcopy",
               "kdma", "tro", "troc", "out", "res",
               "bn2", "aggr2", "var2", "pow2", "va2", "vb2", "pow2b", "y2", "hn2", "tr2", "tr2c", "qkv2", "qkv2c",
               "trk", "kh2", "kl2", "vcopy2", "kdma2", "tro2", "troc2", "out2", "x2", "res2",
               "bn3", "aggr3", "sq3", "var3", "pow3", "xn3", "tr3", "tr3c", "lgt", "lgtc",
               "max", "midx", "midf", "dif", "exp", "den", "w0", "w1", "oh0", "oh1", "cnt", "rank0", "pose", "posm",
               "posd", "posi", "scat"]

        def after(eng, name):
            eng.wait_ge(sem("cls"), CLS.index(name) + 1)

        def cstep(ins, name, check=[0]):
            ins.then_inc(sem("cls"), 1)

        Z = slots[0]

        @block.sync
        def _(sp):
            n_const = 0
            for dst, src in ((small[:], c_small), (ident[:], c_ident), (shift[:], c_shift), (rope[:], c_rope),
                             (w_qkv1[:], wqkv1), (w_out1[:], wout1), (w_qkv2[:], wqkv2), (w_out2[:], wo2),
                             (w_gate[:], gate), (lnw[:, 0], ln1), (lnw[:, 1], ln2),
                             (stage[:, 0:2 * SC], c_masks.rearrange("p a c -> p (a c)")),
                             (taps[:], scharr.rearrange("f o y x -> o (f y x)").partition_broadcast(P)
                              .rearrange("p o (f y x) -> p (o f) y x", f=2, y=3)),
                             (Z.h0[:, 0], cls_tok[0, 0:1, :].partition_broadcast(P).rearrange("p o d -> p (o d)"))):
                sp.dma_start(dst, src).then_inc(sem("const"), 16)
                n_const += 16
            sp.wait_ge(sem("edgew_clear"), 1)
            for f in range(2):
                for side in range(2):
                    dst = edgew[3 * side:3 * side + 3, f, (P - 1) * side:(P - 1) * side + 1]
                    sp.dma_start(dst, scharr[f, 0, 2 * side, :].unsqueeze(1)).then_inc(sem("edgew"), 16)
            sp.wait_ge(sem("mask_s_cast"), 1)
            sp.dma_start(stage[:, 0:2 * TC], c_maskt.rearrange("p a c -> p (a c)")).then_inc(sem("stage2"), 16)
            sp.wait_ge(sem("mask_t_cast"), 1)
            sp.dma_start(stage[:, 0:2 * P], c_prefix).then_inc(sem("stage3"), 16)

            after(sp, "kl")
            for h in range(NH):
                for part, row in ((0, 0), (1, 16), (0, 32), (1, 48)):
                    src = Z.khl[(h % 8) * 16:(h % 8) * 16 + 16, part, h // 8, 0:2].bitcast(F32)
                    sp.dma_start(kst[0][row:row + 16, h, 0:2].bitcast(F32), src).then_inc(sem("kcls1"), 16)
            after(sp, "kl2")
            for h in range(NKV):
                for part, row in ((0, 0), (1, 16), (0, 32), (1, 48)):
                    src = Z.khl[h * 16:h * 16 + 16, part, 0, 0:2].bitcast(F32)
                    sp.dma_start(kst[1][row:row + 16, h, 0:2].bitcast(F32), src).then_inc(sem("kcls2"), 16)

            def load(i, s):
                z = slots[s]
                sp.wait_ge(sem("gray"), i * 2)
                for t in range(NT):
                    src = x[bass.ds(i * 2 + s, 1), :, t * P:(t + 1) * P, :].rearrange("o c p w -> p (o c) w")
                    sp.dma_start(z.xin[:, t], src).then_inc(sem(f"xin{s}"), 16)

            def halo(i, s):
                z = slots[s]
                sp.wait_ge(sem("gray"), i * 2 + s + 1)
                for dx in range(3):
                    sp.dma_start(z.halo[dx:dx + 1, 1], z.gray[P - 1:P, 0, dx:dx + HW]).then_inc(sem(f"halo{s}"), 16)
                    sp.dma_start(z.halo[3 + dx:4 + dx, 0], z.gray[0:1, 1, dx:dx + HW]).then_inc(sem(f"halo{s}"), 16)

            def stack(i, s, a):
                z = slots[s]
                sp.wait_ge(*read(i, s, ("q1", "tr_q2")[a]))
                sp.dma_start(qd[s].rearrange("a m p q -> p (a m) q"),
                             z.qhl[:].rearrange("p a m q -> p (a m) q").bitcast(F32)).then_inc(sem(f"qd{s}"), 16)
                sp.wait_ge(*read(i, s, ("k1", "tr_k2")[a]))
                rows = KV_HEADS[a] * HD // K_TILES[a]
                sp.dma_start(kd[s][:, 0:K_TILES[a], 0:rows].rearrange("a m p q -> p a m q"),
                             z.khl[0:rows, :, 0:K_TILES[a]].bitcast(F32)).then_inc(sem(f"kd{s}"), 16)
                sp.wait_ge(sem(f"qd{s}"), 16 * (2 * i + a + 1))
                for part, row in ((0, 0), (0, 16), (1, 32), (1, 48)):
                    sp.dma_start(qst[row:row + 16].bitcast(F32),
                                 qd[s][part].rearrange("m (h d) q -> d (m h) q", d=HD)).then_inc(sem(f"qst{a}{s}"), 16)
                sp.wait_ge(sem(f"kd{s}"), 16 * (2 * i + a + 1))
                for part, row in ((0, 0), (1, 16), (0, 32), (1, 48)):
                    src = kd[s][part].rearrange("m (h d) q -> d (m h) q", d=HD)[:, 0:KV_HEADS[a]]
                    sp.dma_start(kst[a][row:row + 16, :, 2:KC].bitcast(F32), src).then_inc(sem(f"kst{a}{s}"), 16)

            def maxrows(i, s, a):
                z = slots[s]
                sp.wait_ge(*read(i, s, f"mt{a + 1}"))
                sp.dma_start(md[s], z.mT[:]).then_inc(sem(f"md{s}"), 16)
                sp.wait_ge(sem(f"md{s}"), 16 * (2 * i + a + 1))
                sp.dma_start(qst[64:66].bitcast(F32), md[s].rearrange("(a h) q -> a h q", a=2))\
                    .then_inc(sem(f"mrow{a}{s}"), 16)

            def residual(i, s):
                z = slots[s]
                sp.wait_ge(sem("res"), i * 2 + s + 1)
                sp.dma_start(rs[bass.ds(i * 2 + s, 1)].rearrange("o p d -> p (o d)"),
                             z.res[:].rearrange("p t d -> p (t d)")).then_inc(sem(f"res_saved{s}"), 16)

            with sp.Fori(0, ITERS) as i:
                for s in range(2):
                    load(i, s)
                    halo(i, s)
                    for a in range(2):
                        stack(i, s, a)
                        maxrows(i, s, a)
                    residual(i, s)

            for s in range(2):
                sp.wait_ge(sem(f"scat{s}"), 64 * ITERS)
                sp.wait_ge(sem(f"res_saved{s}"), 16 * ITERS)
                sp.wait_ge(sem("routed"), B)
            sp.dma_start(lnm[:], ln2).then_inc(sem("lnm"), 16)
            for k in range(KT):
                sp.dma_start(w13s[:, k], w13[:, k]).then_inc(sem("w13"), 16)
            sp.dma_start(w2s[:], w2).then_inc(sem("w2"), 16)

            sp.wait_ge(sem("tile_i"), 1)
            sp.wait_ge(sem("zero"), 16 * 2 * NE)
            with sp.Fori(0, MT // 2) as j:
                for n in range(2):
                    sp.wait_ge(sem(f"tr_e{n}"), j)
                    row = sp.value_load(tile_i[0:1, 1, bass.ds(j * 2 + n, 1)], min_val=0, max_val=DUMP - P)
                    sp.dma_start(xt[n][:], hs[bass.ds(row, P), :]).then_inc(sem(f"xt{n}"), 16)
                for n in range(2):
                    sp.wait_ge(sem(f"yo{n}"), j + 1)
                    sp.dma_start(ys[bass.ds((j * 2 + n) * P, P), :], yo[n][:]).then_inc(sem(f"ys{n}"), 16)
            for n in range(2):
                sp.wait_ge(sem(f"ys{n}"), 16 * (MT // 2))
            sp.dma_start(zrow[0:1, 0:1], small[0:1, 0:1]).then_inc(sem("ys_all"), 16)

            with sp.Fori(0, ITERS) as i:
                for s in range(2):
                    sp.wait_ge(sem(f"fo{s}"), i)
                    sp.dma_start(fr[s][:].rearrange("p t d -> p (t d)"),
                                 rs[bass.ds(i * 2 + s, 1)].rearrange("o p d -> p (o d)")).then_inc(sem(f"fr{s}"), 16)
                for s in range(2):
                    sp.wait_ge(sem(f"fo{s}"), i + 1)
                    for t in range(NT):
                        dst = out[bass.ds(i * 2 + s, 1), 1 + t * P:1 + (t + 1) * P, :].rearrange("o p d -> p (o d)")
                        sp.dma_start(dst, fo[s][:, t]).then_inc(sem(f"stored{s}"), 16)
            sp.wait_ge(sem("cls_out"), 1)
            sp.dma_start(out[:, 0, :], fo[0][0:B, 0]).then_inc(sem("stored0"), 16)
            sp.wait_ge(sem("stored0"), 32 * ITERS + 16)
            sp.wait_ge(sem("stored1"), 32 * ITERS)

        @block.gpsimd
        def _(pool):
            pool_engine.append(pool)
            pool.memset(edgew[:], 0.0).then_inc(sem("edgew_clear"), 1)
            for z in slots:
                pool.memset(z.gray[:], 0.0).then_inc(sem("cleared"), 1)
                pool.memset(z.halo[:], 0.0).then_inc(sem("cleared"), 1)
                pool.memset(z.v[0][:], 1.0).then_inc(sem("cleared"), 1)
                pool.memset(z.v[1][:], 1.0).then_inc(sem("cleared"), 1)
            for a in range(2):
                pool.wait_ge(sem("cleared"), 8 + 2 * a)
                pool.memset(kst[a][64:66].bitcast(F32), 1.0).then_inc(sem("cleared"), 1)
                pool.wait_ge(sem("cleared"), 9 + 2 * a)
                pool.memset(vc[a][:], 1.0).then_inc(sem("cleared"), 1)
            pool.wait_ge(sem("const"), 16 * 14)

            def rsqrt(ins, outs, ready, done):
                pool.wait_ge(*ready)
                pool.tensor_tensor(outs, ins, small[:, 53:54].broadcast_to([P, ins.shape[1]]), ALU.pow).then_inc(*done)

            c = sem("cls")
            rsqrt(Z.va[:, 0:1], Z.rstd[:, 0:1], (c, CLS.index("pow")), (c, 1))
            rsqrt(Z.va[:, 0:1], Z.rstd[:, 0:1], (c, CLS.index("pow2")), (c, 1))
            rsqrt(Z.vb[:, 0:1], Z.rr[:, 0:1], (c, CLS.index("pow2b")), (c, 1))
            rsqrt(Z.va[:, 0:1], Z.rr[:, 0:1], (c, CLS.index("pow3")), (c, 1))
            after(pool, "posi")
            for k in range(2):
                pool.indirect_dma_start(out=hs, out_offset=bass.IndirectOffsetOnAxis(ap=Z.pos[:, 0, k:k + 1], axis=0),
                                        in_=Z.xn[:, 0], in_offset=None).then_inc(sem("cls_scat"), 16)

            def rope_half(i, s):
                z = slots[s]
                pool.wait_ge(*read(i, s, "qkv2b"))
                x1, x2 = z.qkv[:, :, 0:20, 0:8], z.qkv[:, :, 0:20, 8:16]
                co = rope[:, 0].unsqueeze(2).broadcast_to([P, NT, 20, 8])
                si = rope[:, 1].unsqueeze(2).broadcast_to([P, NT, 20, 8])
                r2 = z.ra[:, 2].rearrange("p (t h d) -> p t h d", t=NT, h=20)
                r3 = z.ra[:, 3].rearrange("p (t h d) -> p t h d", t=NT, h=20)
                pool.tensor_tensor(r2, x2, co, ALU.mult).then_inc(sem("rope_p"), 1)
                pool.tensor_tensor(r3, x1, si, ALU.mult).then_inc(sem("rope_p"), 1)
                pool.wait_ge(sem("rope_p"), (i * 2 + s) * 3 + 2)
                pool.tensor_tensor(z.rot[:, :, :, 8:16], r2, r3, ALU.add).then_inc(sem("rope_p"), 1)
                pool.tensor_copy(z.v[1][:, :, :, 0:HD], z.qkv[:, :, 20:24, :]).then_inc(sem("v2"), 1)

            def class_value(i, s, a):
                z = slots[s]
                pool.wait_ge(sem(f"pcls{a}"), i * 2 + s + 1)
                for t in range(NT):
                    pool.tensor_tensor(z.ocls[:, t], vc[a][:], z.pcls[:, t].unsqueeze(2).broadcast_to([P, NH, HD + 1]),
                                       ALU.mult).then_inc(sem(f"ocls{a}"), 1)

            def scatter(i, s):
                z = slots[s]
                wait_apart(pool, sem("pos"), i * 2 + s + 1, 1)
                for t in range(NT):
                    for k in range(2):
                        pool.indirect_dma_start(
                            out=hs, out_offset=bass.IndirectOffsetOnAxis(ap=z.pos[:, t, k:k + 1], axis=0),
                            in_=z.xn[:, t], in_offset=None).then_inc(sem(f"scat{s}"), 16)

            with pool.Fori(0, ITERS) as i:
                for s in range(2):
                    z = slots[s]
                    rsqrt(z.va[:], z.rstd[:], (sem("va1"), i * 2 + s + 1), (sem("rstd1"), 1))
                    class_value(i, s, 0)
                    rsqrt(z.va[:], z.rstd[:], (sem("va2"), i * 2 + s + 1), (sem("rstd2"), 1))
                    rsqrt(z.vb[:], z.rr[:], (sem("vb2"), i * 2 + s + 1), (sem("rr2"), 1))
                    rope_half(i, s)
                    class_value(i, s, 1)
                    rsqrt(z.va[:], z.rr[:], (sem("va3"), i * 2 + s + 1), (sem("rr3"), 1))
                    scatter(i, s)

            pool.wait_ge(sem("zpos"), 1)
            for e in range(NE):
                for k in range(2):
                    pool.indirect_dma_start(out=hs, out_offset=bass.IndirectOffsetOnAxis(ap=zpos[:, k, e:e + 1], axis=0),
                                            in_=zrow[:], in_offset=None).then_inc(sem("zero"), 16)

            pool.wait_ge(sem("ys_all"), 16)

            def gather(s, t, k, done):
                pool.indirect_dma_start(out=fy[s][:, t, k], out_offset=None, in_=ys,
                                        in_offset=bass.IndirectOffsetOnAxis(ap=fidx[s][:, t, k:k + 1], axis=0))\
                    .then_inc(done, 16)

            with pool.Fori(0, ITERS) as i:
                for s in range(2):
                    pool.wait_ge(sem(f"idled{s}"), i)
                    wait_apart(pool, sem(f"fidx{s}"), i + 1, 2 + s).then_inc(sem(f"idled{s}"), 1)
                    for t in range(NT):
                        for k in range(2):
                            gather(s, t, k, sem(f"fy{s}"))
            pool.wait_ge(sem("cls_fidx"), 1)
            for k in range(2):
                gather(0, 0, k, sem("cls_fy"))

        @block.scalar
        def _(act):
            act.wait_ge(sem("const"), 16 * 14)

            def ccopy(dst, src, name, before):
                after(act, before)
                act.activation(dst, src, ACT.Copy).then_inc(sem("cls"), 1)

            fb = bank[6]
            for (name, before) in (("trc", "tr"), ("troc", "tro"), ("tr2c", "tr2"), ("qkv2c", "qkv2"),
                                   ("troc2", "tro2"), ("tr3c", "tr3")):
                if name == "qkv2c":
                    ccopy(Z.qkv[:, 0], fb[:, 0:384], name, before)
                else:
                    ccopy(Z.yT[:, :, 0:P], fb[:, 0:2 * P], name, before)
            after(act, "dif")
            act.activation(Z.ew[:, 0, 0:1], Z.ew[:, 0, 0:1], ACT.Exp).then_inc(sem("cls"), 1)

            def edges(i, s):
                z = slots[s]
                act.wait_ge(*written(i, s, "conv0"))
                act.activation(z.h0[:], gbank(s, "conv0")[:], ACT.Abs, scale=0.5).then_inc(read_sem(s, "conv0"), 1)
                act.wait_ge(*written(i, s, "conv1"))
                act.activation(z.tmp[:], gbank(s, "conv1")[:], ACT.Abs, scale=0.5).then_inc(read_sem(s, "conv1"), 1)

            def take(i, s, g, dst, src, scale=1.0):
                act.wait_ge(*written(i, s, g))
                act.activation(dst, src, ACT.Copy, scale=scale).then_inc(read_sem(s, g), 1)

            def high(i, s, a, g, key, dst, src, scale):
                act.wait_ge(*written(i, s, g))
                act.activation(dst, src, ACT.Copy, scale=scale).then_inc(sem(f"{key}hi{a}"), 1)

            def attention(i, s, a):
                z = slots[s]
                take(i, s, f"mt{a + 1}", z.mT[:], gbank(s, f"mt{a + 1}")[0:32, 0:2 * P])
                act.wait_ge(sem(f"dcls{a}"), i * 2 + s + 1)
                act.activation(z.pcls[:], z.pcls[:], ACT.Exp).then_inc(sem(f"pcls{a}"), 1)
                for p in range(PAIRS):
                    act.wait_ge(sem(f"st{a}"), (i * 2 + s) * PAIRS + p + 1)
                    if p >= 2:
                        act.wait_ge(sem(f"pv{a}"), (i * 2 + s) * PAIRS + p - 1)
                    for u in range(2):
                        src = bank[2 * (p % 2) + u][:, 0:TC]
                        ins = act.activation(prob[p % 2][:, u], src, ACT.Exp)
                    ins.then_inc(sem(f"exp{a}"), 1)

            with act.Fori(0, ITERS) as i:
                for s in range(2):
                    z = slots[s]
                    full = lambda g: gbank(s, g)[:].rearrange("p (k q) -> p k q", k=2)
                    edges(i, s)
                    take(i, s, "tr_y1", z.yT[:], full("tr_y1"))
                    high(i, s, 0, "q1", "q", z.qhl[:, 0], full("q1"), 0.25)
                    high(i, s, 0, "k1", "k", z.khl[:, 0], full("k1"), 1.0)
                    act.wait_ge(*written(i, s, "v1"))
                    for t in range(NT):
                        ins = act.activation(z.v[0][:, t, :, 0:HD],
                                             full("v1")[:, t].rearrange("p (h d) -> p h d", h=NH), ACT.Copy)
                    ins.then_inc(read_sem(s, "v1"), 1)
                    attention(i, s, 0)
                    take(i, s, "tr_o1", z.yT[:], full("tr_o1"))
                    take(i, s, "tr_y2", z.yT[:], full("tr_y2"))
                    for t, g in enumerate(("qkv2a", "qkv2b")):
                        take(i, s, g, z.qkv[:, t].rearrange("p h d -> p (h d)"), gbank(s, g)[:, 0:384])
                    high(i, s, 1, "tr_q2", "q", z.qhl[:, 0], full("tr_q2"), 0.25)
                    high(i, s, 1, "tr_k2", "k", z.khl[0:64, 0, 0], gbank(s, "tr_k2")[0:64, 0:256], 1.0)
                    attention(i, s, 1)
                    take(i, s, "tr_o2", z.yT[:], full("tr_o2"))
                    take(i, s, "tr_x", z.yT[:], full("tr_x"))
                    act.wait_ge(sem("dtop"), i * 2 + s + 1)
                    act.activation(z.ew[:, :, 0], z.ew[:, :, 0], ACT.Exp).then_inc(sem("etop"), 1)

            with act.Fori(0, MT // 2) as j:
                for n in range(2):
                    act.wait_ge(sem(f"tr_e{n}"), j + 1)
                    act.wait_ge(sem(f"up{n}"), j)
                    act.activation(xT[n][:], bank[0][:, 0:2 * P], ACT.Copy).then_inc(sem(f"xT{n}"), 1)
                    act.wait_ge(sem(f"up{n}"), j + 1)
                    act.activation(sg[n][:], bank[2 + 2 * n][:], ACT.Silu).then_inc(sem(f"silu{n}"), 1)
                    act.wait_ge(sem(f"tr_g{n}"), j + 1)
                    act.activation(guT[n][:], bank[6][:], ACT.Copy).then_inc(sem(f"guT{n}"), 1)

        @block.tensor
        def _(pe):
            pe.wait_ge(sem("const"), 16 * 14)

            def transpose_blocks(dst, src, cols):
                return pe.transpose(dst, src, ident[:])

            def cmm(name, before, groups):
                after(pe, before)
                for dst, pairs in groups:
                    for n, (lt, rh) in enumerate(pairs):
                        ins = pe.matmul(dst, lt, rh, start=(n == 0), stop=(n == len(pairs) - 1))
                ins.then_inc(sem("cls"), 1)

            def ctr(name, before, src, cols=(P, P)):
                after(pe, before)
                for n, c in enumerate(cols):
                    ins = pe.transpose(fb[0:c, n * P:(n + 1) * P], src[:, n * P:n * P + c], ident[:])
                ins.then_inc(sem("cls"), 1)

            fb, fc, fd = bank[6], bank[7], bank[4]
            fk = [(Z.yT[:, k, 0:P]) for k in range(KT)]
            ctr("tr", "ln", Z.y[:, 0])
            cmm("qkv", "trc",
                [(fc[:, 0:D], [(fk[k], w_qkv1[:, k, 2 * D:3 * D]) for k in range(KT)])]
                + [(fd[:, m * P:(m + 1) * P], [(w_qkv1[:, k, D + m * P:D + (m + 1) * P], fk[k]) for k in range(KT)])
                   for m in range(2)])
            ctr("tro", "kdma", Z.tmp[:, 0])
            cmm("out", "troc", [(fc[:, 0:D], [(fk[k], w_out1[:, k]) for k in range(KT)])])
            ctr("tr2", "hn2", Z.hn[:, 0])
            pe.wait_ge(sem("scaled_w"), 1)
            cmm("qkv2", "tr2c", [(fb[:, 0:384], [(fk[k], w_qkv2[:, k]) for k in range(KT)])])
            after(pe, "qkv2c")
            pe.transpose(fd[0:64, 0:P], Z.qkv[:, 0, 16:20, :].rearrange("p h d -> p (h d)"), ident[:])\
                .then_inc(sem("cls"), 1)
            ctr("tro2", "kdma2", Z.tmp[:, 0])
            cmm("out2", "troc2", [(fc[:, 0:D], [(fk[k], w_out2[:, k]) for k in range(KT)])])
            ctr("tr3", "xn3", Z.xn[:, 0])
            cmm("lgt", "tr3c", [(fc[:, 0:NE], [(fk[k], w_gate[:, k]) for k in range(KT)])])
            after(pe, "scat")
            pe.wait_ge(sem("masks"), 3)
            pe.wait_ge(sem("bands"), 1)
            pe.wait_ge(sem("edgew"), 64)
            pe.wait_ge(sem("kcls1"), 16 * 4 * NH)
            pe.wait_ge(sem("kcls2"), 16 * 4 * NKV)
            pe.wait_ge(sem("cleared"), 12)

            def conv(i, s):
                z = slots[s]
                for f in range(2):
                    g_free(pe, i, s, f"conv{f}")
                    if f == 0:
                        pe.wait_ge(sem("gray"), i * 2 + s + 1)
                    for dx in range(3):
                        pe.matmul(gbank(s, f"conv{f}")[:], band[:, f, dx], z.gray[:, :, dx:dx + HW],
                                  start=(dx == 0), stop=False)
                    if f == 0:
                        pe.wait_ge(sem(f"halo{s}"), 16 * 6 * (i + 1))
                    pe.matmul(gbank(s, f"conv{f}")[:], edgew[:, f], z.halo[:], start=False, stop=True)\
                        .then_inc(sem("g_written"), 1)

            def tr(i, s, g, src, ready):
                g_free(pe, i, s, g)
                pe.wait_ge(sem(ready), i * 2 + s + 1)
                for k in range(KT):
                    for t in range(NT):
                        c = k * 2 * P + t * P
                        ins = pe.transpose(gbank(s, g)[:, c:c + P], src[:, t, k * P:(k + 1) * P], ident[:])
                ins.then_inc(sem("g_written"), 1)

            def project_T(i, s, g, w, c0):
                g_free(pe, i, s, g)
                for m in range(2):
                    for k in range(KT):
                        ins = pe.matmul(gbank(s, g)[:, m * 2 * P:(m + 1) * 2 * P],
                                        w[:, k, c0 + m * P:c0 + (m + 1) * P], slots[s].yT[:, k],
                                        start=(k == 0), stop=(k == KT - 1))
                ins.then_inc(sem("g_written"), 1)

            def project(i, s, g, w, c0):
                g_free(pe, i, s, g)
                for t in range(NT):
                    for k in range(KT):
                        ins = pe.matmul(gbank(s, g)[:, t * D:(t + 1) * D], slots[s].yT[:, k, t * P:(t + 1) * P],
                                        w[:, k, c0:c0 + D], start=(k == 0), stop=(k == KT - 1))
                ins.then_inc(sem("g_written"), 1)

            def attention(i, s, a):
                z = slots[s]
                rep = (1, NH // NKV)[a]
                before = i * 2 + s + a

                pe.wait_ge(sem(f"qst{a}{s}"), 16 * 4 * (i + 1))
                pe.wait_ge(sem(f"kst{a}{s}"), 16 * 4 * (i + 1))
                pe.wait_ge(sem(f"exp{1 - a}"), before * PAIRS)
                for p in range(PAIRS):
                    if p >= 2:
                        pe.wait_ge(sem(f"max{a}"), (i * 2 + s) * PAIRS + p - 1)
                    for u in range(2):
                        h = 2 * p + u
                        o = bank[2 * (p % 2) + u]
                        pe.matmul(o[:, 0:SC], identb[:], mask_s[:, a], start=True, stop=False)
                        pe.matmul(o[:, 0:QC], qst[0:64, h, 0:P], kst[a][0:64, h // rep, 0:QC],
                                  start=False, stop=False)
                        ins = pe.matmul(o[:, QC:SC], qst[0:64, h, P:2 * P], kst[a][0:64, h // rep, :],
                                        start=False, stop=True)
                    ins.then_inc(sem(f"s{a}"), 1)
                g_free(pe, i, s, f"mt{a + 1}")
                pe.wait_ge(sem(f"nm{a}"), i * 2 + s + 1)
                for t in range(NT):
                    ins = pe.transpose(gbank(s, f"mt{a + 1}")[0:32, t * P:(t + 1) * P],
                                       z.nm[:, t].rearrange("p a h -> p (a h)").bitcast(F32), ident[:])
                ins.then_inc(sem("g_written"), 1)

                def values(p):
                    pe.wait_ge(sem(f"exp{a}"), (i * 2 + s) * PAIRS + p + 1)
                    for u in range(2):
                        h = 2 * p + u
                        w = prob[p % 2][:, u]
                        c = slice(h * (HD + 1), (h + 1) * (HD + 1))
                        pe.matmul(bank[4][:, c], w[:, 0:P], z.v[a][:, 0, h // rep], start=True, stop=True)
                        pe.matmul(bank[5][:, c], w[:, P:2 * P], z.v[a][:, 0, h // rep], start=True, stop=False)
                        ins = pe.matmul(bank[5][:, c], w[:, 2 * P:TC], z.v[a][:, 1, h // rep], start=False, stop=True)
                    ins.then_inc(sem(f"pv{a}"), 1)

                pe.wait_ge(sem(f"mrow{a}{s}"), 16 * (i + 1))
                pe.wait_ge(sem(f"osum{1 - a}"), before * NT)
                if a == 0:
                    pe.wait_ge(*read(i, s, "v1"))
                else:
                    pe.wait_ge(sem("v2"), i * 2 + s + 1)
                for p in range(PAIRS):
                    if p < 2:
                        pe.wait_ge(sem(f"max{a}"), (i * 2 + s) * PAIRS + PAIRS - 1 + p)
                    else:
                        pe.wait_ge(sem(f"exp{a}"), (i * 2 + s) * PAIRS + p - 1)
                    for u in range(2):
                        h = 2 * p + u
                        o = bank[2 * (p % 2) + u]
                        pe.matmul(o[:, 0:TC], identb[:], mask_t[:, a], start=True, stop=False)
                        pe.matmul(o[:, 0:2 * P], kst[a][0:66, h // rep, 2:P + 2], qst[0:66, h], start=False, stop=False)
                        ins = pe.matmul(o[:, 2 * P:TC], kst[a][0:66, h // rep, P + 2:KC], qst[0:66, h, P:2 * P],
                                        start=False, stop=True)
                    ins.then_inc(sem(f"st{a}"), 1)
                    if p >= 1:
                        values(p - 1)
                values(PAIRS - 1)

            with pe.Fori(0, ITERS) as i:
                for s in range(2):
                    z = slots[s]
                    conv(i, s)
                    tr(i, s, "tr_y1", z.y, "ln1")
                    pe.wait_ge(*read(i, s, "tr_y1"))
                    project_T(i, s, "q1", w_qkv1, 0)
                    project_T(i, s, "k1", w_qkv1, D)
                    project(i, s, "v1", w_qkv1, 2 * D)
                    attention(i, s, 0)
                    tr(i, s, "tr_o1", z.tmp, "on0")
                    pe.wait_ge(*read(i, s, "tr_o1"))
                    project(i, s, "out1", w_out1, 0)
                    tr(i, s, "tr_y2", z.hn, "hn")
                    pe.wait_ge(*read(i, s, "tr_y2"))
                    for t, g in enumerate(("qkv2a", "qkv2b")):
                        g_free(pe, i, s, g)
                        for k in range(KT):
                            ins = pe.matmul(gbank(s, g)[:, 0:384], z.yT[:, k, t * P:(t + 1) * P], w_qkv2[:, k],
                                            start=(k == 0), stop=(k == KT - 1))
                        ins.then_inc(sem("g_written"), 1)
                    g_free(pe, i, s, "tr_q2")
                    pe.wait_ge(sem("rope_p"), (i * 2 + s) * 3 + 3)
                    pe.wait_ge(sem("rope_v"), (i * 2 + s) * 3 + 3)
                    rot = z.rot[:].rearrange("p t h d -> p t (h d)")
                    for m in range(2):
                        for t in range(NT):
                            ins = pe.transpose(gbank(s, "tr_q2")[:, m * 2 * P + t * P:m * 2 * P + (t + 1) * P],
                                               rot[:, t, m * P:(m + 1) * P], ident[:])
                    ins.then_inc(sem("g_written"), 1)
                    pe.wait_ge(sem("const"), 16 * 14)
                    g_free(pe, i, s, "tr_k2")
                    for t in range(NT):
                        ins = pe.transpose(gbank(s, "tr_k2")[0:64, t * P:(t + 1) * P], rot[:, t, D:D + 64], ident[:])
                    ins.then_inc(sem("g_written"), 1)
                    attention(i, s, 1)
                    tr(i, s, "tr_o2", z.tmp, "on1")
                    pe.wait_ge(*read(i, s, "tr_o2"))
                    project(i, s, "out2", w_out2, 0)
                    tr(i, s, "tr_x", z.xn, "xn")
                    pe.wait_ge(*read(i, s, "tr_x"))
                    g_free(pe, i, s, "lgt")
                    for t in range(NT):
                        for k in range(KT):
                            ins = pe.matmul(gbank(s, "lgt")[:, t * NE:(t + 1) * NE], z.yT[:, k, t * P:(t + 1) * P],
                                            w_gate[:, k], start=(k == 0), stop=(k == KT - 1))
                    ins.then_inc(sem("g_written"), 1)
                    g_free(pe, i, s, "rank")
                    pe.wait_ge(sem("pick"), i * 2 + s + 1)
                    gb = gbank(s, "rank")
                    pe.matmul(gb[:, 0:NE], prefix[:, 0], z.pick[:, 0], start=True, stop=True)
                    for c, ops in ((1, ((0, 1), (1, 0))), (2, ((1, 1), (1, 0)))):
                        first = prefix[:, 0] if c == 1 else prefix[:, 1]
                        pe.matmul(gb[:, c * NE:(c + 1) * NE], first, z.pick[:, 1], start=True, stop=False)
                        ins = pe.matmul(gb[:, c * NE:(c + 1) * NE], prefix[:, 1], z.pick[:, 0], start=False, stop=True)
                    ins.then_inc(sem("g_written"), 1)

            pe.wait_ge(sem("w13_scaled"), KT * NE)
            pe.wait_ge(sem("w2"), 16)
            with pe.Fori(0, MT // 2) as j:
                for n in range(2):
                    e = pe.value_load(tile_i[0:1, 0, bass.ds(j * 2 + n, 1)], min_val=0, max_val=NE - 1)
                    pe.wait_ge(sem(f"xt{n}"), 16 * (j + 1))
                    pe.wait_ge(sem(f"xT{1 - n}"), j + n)
                    for k in range(KT):
                        ins = pe.transpose(bank[0][:, k * P:(k + 1) * P], xt[n][:, k * P:(k + 1) * P], ident[:])
                    ins.then_inc(sem(f"tr_e{n}"), 1)
                    pe.wait_ge(sem(f"xT{n}"), j + 1)
                    pe.wait_ge(sem(f"gu{n}"), j)
                    for half in range(2):
                        for k in range(KT):
                            ins = pe.matmul(bank[2 + 2 * n + half][:], xT[n][:, k],
                                            w13s[:, k, bass.ds(e, 1), half * FFN:(half + 1) * FFN],
                                            start=(k == 0), stop=(k == KT - 1))
                    ins.then_inc(sem(f"up{n}"), 1)
                    pe.wait_ge(sem(f"gu{n}"), j + 1)
                    pe.wait_ge(sem(f"guT{1 - n}"), j + n)
                    for f in range(FT):
                        ins = pe.transpose(bank[6][:, f * P:(f + 1) * P], gu[n][:, f * P:(f + 1) * P], ident[:])
                    ins.then_inc(sem(f"tr_g{n}"), 1)
                    pe.wait_ge(sem(f"guT{n}"), j + 1)
                    pe.wait_ge(sem(f"yo{1 - n}"), j + n)
                    for f in range(FT):
                        ins = pe.matmul(bank[7][:, 0:D], guT[n][:, f], w2s[:, f, bass.ds(e, 1), :],
                                        start=(f == 0), stop=(f == FT - 1))
                    ins.then_inc(sem(f"down{n}"), 1)

        @block.vector
        def _(dve):
            dve.wait_ge(sem("const"), 16 * 14)
            chain = [0]

            def link(ins):
                chain[0] += 1
                ins.then_inc(sem("dve_chain"), 1)
                dve.wait_ge(sem("dve_chain"), chain[0])

            dve.tensor_copy(mask_s[:].rearrange("p a c -> p (a c)"), stage[:, 0:2 * SC]).then_inc(sem("mask_s_cast"), 1)
            dve.tensor_copy(identb[:], ident[:]).then_inc(sem("masks"), 1)
            dve.wait_ge(sem("stage2"), 16)
            dve.tensor_copy(mask_t[:].rearrange("p a c -> p (a c)"), stage[:, 0:2 * TC]).then_inc(sem("mask_t_cast"), 1)
            dve.wait_ge(sem("stage3"), 16)
            dve.tensor_copy(prefix[:].rearrange("p a c -> p (a c)"), stage[:, 0:2 * P]).then_inc(sem("masks"), 2)
            for f in range(2):
                for dx in range(3):
                    link(dve.tensor_scalar(band[:, f, dx], shift[:, 0], taps[:, f, 0, dx:dx + 1], None, ALU.mult))
                    for dy in range(1, 3):
                        link(dve.scalar_tensor_tensor(out=band[:, f, dx], in0=shift[:, dy],
                                                      scalar=taps[:, f, dy, dx:dx + 1], in1=band[:, f, dx],
                                                      op0=ALU.mult, op1=ALU.add))
            for k in range(KT):
                link(dve.tensor_scalar(w_qkv2[:, k], w_qkv2[:, k], lnw[:, 0, k:k + 1], None, ALU.mult))
                link(dve.tensor_scalar(w_gate[:, k], w_gate[:, k], lnw[:, 1, k:k + 1], None, ALU.mult))
            dve.tensor_scalar(Z.va[:, 1:2], small[:, 0:1], 0.0, None, ALU.mult).then_inc(sem("bands"), 1)
            dve.tensor_scalar(Z.vb[:, 1:2], small[:, 0:1], 0.0, None, ALU.mult).then_inc(sem("scaled_w"), 1)

            c = sem("cls")
            dve.wait_ge(sem("cleared"), 12)
            dve.wait_ge(sem("mask_t_cast"), 1)
            dve.tensor_copy(Z.rr[:, 0:1], small[:, 41:42]).then_inc(c, 1)
            dve.tensor_copy(Z.rr[:, 1:2], small[:, 41:42]).then_inc(c, 1)

            def d(name, f, *args, **kw):
                dve.wait_ge(c, CLS.index(name))
                f(*args, **kw).then_inc(c, 1)

            def cstats(x, n):
                d("bn" + n, dve.bn_stats, Z.bn[:, 0], x)
                d("aggr" + n, dve.bn_aggr, Z.st[:, 0], Z.bn[:, 0])

            cstats(Z.h0[:, 0], "")
            d("var", dve.tensor_scalar, Z.va[:, 0:1], Z.st[:, 0, 1:2], EPS, None, ALU.add)
            d("ln", dve.tensor_scalar, Z.y[:, 0], Z.h0[:, 0], Z.st[:, 0, 0:1], Z.rstd[:, 0:1], ALU.subtract, ALU.mult)
            kps = bank[4][:, 0:2 * P].rearrange("p (m q) -> p m q", m=2)[:, :, 0:2]
            d("kh", dve.tensor_copy, Z.khl[:, 0, :, 0:2], kps)
            d("kl", dve.tensor_tensor, Z.khl[:, 1, :, 0:2], kps, Z.khl[:, 0, :, 0:2].bitcast(F32), ALU.subtract)
            vps = bank[7][:, 0:D].rearrange("p (h d) -> p h d", h=NH)
            d("vcopy", dve.tensor_copy, vc[0][:, :, 0:HD], vps)
            d("kdma", dve.tensor_copy, Z.tmp[:, 0].rearrange("p (h d) -> p h d", h=NH), vc[0][:, :, 0:HD])
            d("res", dve.tensor_tensor, Z.h0[:, 0], Z.h0[:, 0], bank[7][:, 0:D], ALU.add)
            cstats(Z.h0[:, 0], "2")
            d("var2", dve.tensor_scalar, Z.va[:, 0:1], Z.st[:, 0, 1:2], EPS, None, ALU.add)
            d("va2", dve.tensor_tensor, Z.vb[:, 0:1], Z.rstd[:, 0:1], Z.rstd[:, 0:1], ALU.mult)
            d("vb2", dve.tensor_scalar, Z.vb[:, 0:1], Z.vb[:, 0:1], Z.st[:, 0, 1:2], EPS, ALU.mult, ALU.add)
            d("y2", dve.tensor_scalar, Z.y[:, 0], Z.h0[:, 0], Z.st[:, 0, 0:1], Z.rstd[:, 0:1], ALU.subtract, ALU.mult)
            d("hn2", dve.tensor_scalar, Z.hn[:, 0], Z.y[:, 0], Z.rr[:, 0:1], None, ALU.mult)
            kps2 = bank[4][0:64, 0:2]
            dve.wait_ge(sem("kcls1"), 16 * 4 * NH)
            d("kh2", dve.tensor_copy, Z.khl[0:64, 0, 0, 0:2], kps2)
            d("kl2", dve.tensor_tensor, Z.khl[0:64, 1, 0, 0:2], kps2, Z.khl[0:64, 0, 0, 0:2].bitcast(F32), ALU.subtract)
            d("vcopy2", dve.tensor_copy, vc[1][:, :, 0:HD].rearrange("p (g r) d -> p g r d", g=NKV),
              Z.qkv[:, 0, 20:24, :].unsqueeze(2).broadcast_to([P, NKV, NH // NKV, HD]))
            d("kdma2", dve.tensor_copy, Z.tmp[:, 0].rearrange("p (h d) -> p h d", h=NH), vc[1][:, :, 0:HD])
            d("x2", dve.tensor_tensor, Z.y[:, 0], Z.y[:, 0], bank[7][:, 0:D], ALU.add)
            d("res2", dve.tensor_tensor, cls_res[:], Z.y[:, 0], Z.h0[:, 0], ALU.add)
            cstats(Z.y[:, 0], "3")
            d("sq3", dve.tensor_tensor, Z.vb[:, 0:1], Z.st[:, 0, 0:1], Z.st[:, 0, 0:1], ALU.mult)
            d("var3", dve.tensor_scalar, Z.va[:, 0:1], Z.vb[:, 0:1], Z.st[:, 0, 1:2], EPS, ALU.add, ALU.add)
            d("xn3", dve.tensor_scalar, Z.xn[:, 0], Z.y[:, 0], Z.rr[:, 0:1], None, ALU.mult)
            ro = route[:, RT - 1]
            d("lgtc", dve.tensor_copy, Z.lg[:, 0], bank[7][:, 0:NE])
            d("max", dve.max, Z.top[:, 0], Z.lg[:, 0])
            d("midx", dve.max_index, Z.idx[:, 0], Z.top[:, 0], Z.lg[:, 0])
            d("midf", dve.tensor_copy, ro[:, 0:2], Z.idx[:, 0, 0:2])
            d("dif", dve.tensor_tensor, Z.ew[:, 0, 0:1], Z.top[:, 0, 1:2], Z.top[:, 0, 0:1], ALU.subtract)
            d("den", dve.tensor_scalar, Z.ew[:, 0, 1:2], Z.ew[:, 0, 0:1], 1.0, None, ALU.add)
            d("w0", dve.reciprocal, ro[:, 4:5], Z.ew[:, 0, 1:2])
            d("w1", dve.tensor_tensor, ro[:, 5:6], Z.ew[:, 0, 0:1], ro[:, 4:5], ALU.mult)
            for k in range(2):
                d(f"oh{k}", dve.tensor_scalar, Z.oh[:, 0, k], small[:, 0:8], ro[:, k:k + 1], None, ALU.is_equal)
            d("cnt", dve.tensor_tensor, counts[:], Z.oh[:, 0, 0], Z.oh[:, 0, 1], ALU.add)
            d("rank0", dve.memset, ro[:, 2:4], 0.0)
            d("pose", dve.tensor_scalar, Z.posf[:, 0], ro[:, 0:2], float(REGION), None, ALU.mult)
            d("posm", dve.tensor_scalar, Z.posf[:, 0], Z.posf[:, 0], small[:, 42:43], None, ALU.mult)
            d("posd", dve.tensor_tensor, Z.posf[:, 0], Z.posf[:, 0], small[:, 43:45], ALU.add)
            d("posi", dve.tensor_copy, Z.pos[:, 0], Z.posf[:, 0])
            dve.wait_ge(sem("cls_scat"), 32)
            dve.wait_ge(c, CLS.index("scat"))
            dve.tensor_copy(Z.va[:, 0:1], small[:, 0:1]).then_inc(c, 1)
            dve.wait_ge(sem("kcls1"), 16 * 4 * NH)
            dve.wait_ge(sem("kcls2"), 16 * 4 * NKV)

            place, own_count = {}, 2 * OWN_STEPS

            def made(s, name):
                place[s, name] = len(place) + 1
                return sem("vector_own"), 1

            def own(i, s, name):
                return sem("vector_own"), i * own_count + place[s, name]

            def gray(i, s):
                z = slots[s]
                dve.wait_ge(sem(f"xin{s}"), 32 * (i + 1))
                g = z.gray[:, :, 1:HW + 1]
                dve.wait_ge(sem(f"halo{s}"), 96 * i)
                dve.tensor_scalar(g, z.xin[:, :, 0], GRAY[0], None, ALU.mult).then_inc(*made(s, "g1"))
                dve.wait_ge(*own(i, s, "g1"))
                dve.scalar_tensor_tensor(out=g, in0=z.xin[:, :, 1], scalar=GRAY[1], in1=g, op0=ALU.mult,
                                         op1=ALU.add).then_inc(*made(s, "g2"))
                dve.wait_ge(*own(i, s, "g2"))
                dve.scalar_tensor_tensor(out=g, in0=z.xin[:, :, 2], scalar=GRAY[2], in1=g, op0=ALU.mult,
                                         op1=ALU.add).then_inc(sem("gray"), 1)

            def stats(i, s, n, x, ready):
                z = slots[s]
                dve.wait_ge(*ready)
                for t in range(NT):
                    ins = dve.bn_stats(z.bn[:, t], x[:, t])
                ins.then_inc(*made(s, f"bn{n}"))
                wait_apart(dve, *own(i, s, f"bn{n}"), 0)
                for t in range(NT):
                    ins = dve.bn_aggr(z.st[:, t], z.bn[:, t])
                ins.then_inc(*made(s, f"st_{n}"))
                dve.wait_ge(*own(i, s, f"st_{n}"))

            def lowpart(i, s, a, g, key, dst, src, hi, scale):
                dve.wait_ge(sem(f"{key}hi{a}"), i * 2 + s + 1)
                dve.scalar_tensor_tensor(out=dst, in0=src, scalar=scale, in1=hi.bitcast(F32), op0=ALU.mult,
                                         op1=ALU.subtract).then_inc(read_sem(s, g), 1)

            def attention(i, s, a):
                z = slots[s]
                for p in range(PAIRS):
                    dve.wait_ge(sem(f"s{a}"), (i * 2 + s) * PAIRS + p + 1)
                    for u in range(2):
                        h = 2 * p + u
                        o = bank[2 * (p % 2) + u]
                        dve.tensor_copy(z.scls[:, :, h], o[:, 0:QC + 1:QC])
                        dve.tensor_reduce(z.mx[:, 0, h:h + 1], o[:, 0:QC], AX.X, ALU.max)
                        ins = dve.tensor_reduce(z.mx[:, 1, h:h + 1], o[:, QC:SC], AX.X, ALU.max)
                    ins.then_inc(sem(f"max{a}"), 1)
                dve.wait_ge(sem(f"max{a}"), (i * 2 + s + 1) * PAIRS)
                dve.tensor_scalar(z.nm[:, :, 0], z.mx[:], -1.0, None, ALU.mult).then_inc(*made(s, f"nmh{a}"))
                dve.tensor_tensor(z.pcls[:], z.scls[:], z.mx[:], ALU.subtract).then_inc(sem(f"dcls{a}"), 1)
                dve.wait_ge(*own(i, s, f"nmh{a}"))
                dve.scalar_tensor_tensor(out=z.nm[:, :, 1], in0=z.mx[:], scalar=-1.0, in1=z.nm[:, :, 0].bitcast(F32),
                                         op0=ALU.mult, op1=ALU.subtract).then_inc(sem(f"nm{a}"), 1)
                dve.wait_ge(sem(f"pv{a}"), (i * 2 + s + 1) * PAIRS)
                dve.wait_ge(sem(f"ocls{a}"), (i * 2 + s + 1) * NT)
                for t in range(NT):
                    dve.tensor_tensor(z.osum[:, t].rearrange("p h d -> p (h d)"), bank[4 + t][:, 0:NH * (HD + 1)],
                                      z.ocls[:, t].rearrange("p h d -> p (h d)"), ALU.add)\
                        .then_inc(sem(f"osum{a}"), 1)
                dve.wait_ge(sem(f"osum{a}"), (i * 2 + s + 1) * NT)
                dve.reciprocal(z.rden[:], z.osum[:, :, :, HD]).then_inc(*made(s, f"rden{a}"))
                dve.wait_ge(*own(i, s, f"rden{a}"))
                dve.tensor_tensor(z.tmp[:].rearrange("p t (h d) -> p t h d", h=NH), z.osum[:, :, :, 0:HD],
                                  z.rden[:].unsqueeze(3).broadcast_to([P, NT, NH, HD]), ALU.mult)\
                    .then_inc(sem(f"on{a}"), 1)

            def batch(i, s):
                z = slots[s]
                full = lambda g: gbank(s, g)[:].rearrange("p (k q) -> p k q", k=2)
                gray(i, s)
                dve.wait_ge(*read(i, s, "conv0"))
                dve.wait_ge(*read(i, s, "conv1"))
                dve.tensor_tensor(z.h0[:], z.h0[:], z.tmp[:], ALU.add).then_inc(sem("h0"), 1)
                stats(i, s, 1, z.h0, (sem("h0"), i * 2 + s + 1))
                dve.tensor_scalar(z.va[:], z.st[:, :, 1], EPS, None, ALU.add).then_inc(sem("va1"), 1)
                dve.wait_ge(sem("rstd1"), i * 2 + s + 1)
                for t in range(NT):
                    ins = dve.tensor_scalar(z.y[:, t], z.h0[:, t], z.st[:, t, 0:1], z.rstd[:, t:t + 1],
                                            ALU.subtract, ALU.mult)
                ins.then_inc(sem("ln1"), 1)
                lowpart(i, s, 0, "q1", "q", z.qhl[:, 1], full("q1"), z.qhl[:, 0], 0.25)
                lowpart(i, s, 0, "k1", "k", z.khl[:, 1], full("k1"), z.khl[:, 0], 1.0)
                attention(i, s, 0)
                dve.wait_ge(*written(i, s, "out1"))
                dve.tensor_tensor(z.h0[:], z.h0[:], full("out1"), ALU.add).then_inc(read_sem(s, "out1"), 1)
                stats(i, s, 2, z.h0, read(i, s, "out1"))
                dve.tensor_scalar(z.va[:], z.st[:, :, 1], EPS, None, ALU.add).then_inc(sem("va2"), 1)
                dve.wait_ge(sem("rstd2"), i * 2 + s + 1)
                dve.tensor_tensor(z.vb[:], z.rstd[:], z.rstd[:], ALU.mult).then_inc(*made(s, "vr"))
                for t in range(NT):
                    ins = dve.tensor_scalar(z.y[:, t], z.h0[:, t], z.st[:, t, 0:1], z.rstd[:, t:t + 1],
                                            ALU.subtract, ALU.mult)
                ins.then_inc(*made(s, "y2"))
                dve.wait_ge(*own(i, s, "vr"))
                dve.tensor_tensor(z.vb[:], z.vb[:], z.st[:, :, 1], ALU.mult).then_inc(*made(s, "vs"))
                dve.wait_ge(*own(i, s, "vs"))
                dve.tensor_scalar(z.vb[:], z.vb[:], EPS, None, ALU.add).then_inc(sem("vb2"), 1)
                dve.wait_ge(*own(i, s, "y2"))
                dve.wait_ge(sem("rr2"), i * 2 + s + 1)
                for t in range(NT):
                    ins = dve.tensor_scalar(z.hn[:, t], z.y[:, t], z.rr[:, t:t + 1], None, ALU.mult)
                ins.then_inc(sem("hn"), 1)
                dve.wait_ge(*read(i, s, "qkv2b"))
                x1, x2 = z.qkv[:, :, 0:20, 0:8], z.qkv[:, :, 0:20, 8:16]
                co = rope[:, 0].unsqueeze(2).broadcast_to([P, NT, 20, 8])
                si = rope[:, 1].unsqueeze(2).broadcast_to([P, NT, 20, 8])
                r0 = z.ra[:, 0].rearrange("p (t h d) -> p t h d", t=NT, h=20)
                r1 = z.ra[:, 1].rearrange("p (t h d) -> p t h d", t=NT, h=20)
                dve.tensor_tensor(r0, x1, co, ALU.mult).then_inc(sem("rope_v"), 1)
                dve.tensor_tensor(r1, x2, si, ALU.mult).then_inc(sem("rope_v"), 1)
                dve.wait_ge(sem("rope_v"), (i * 2 + s) * 3 + 2)
                dve.tensor_tensor(z.rot[:, :, :, 0:8], r0, r1, ALU.subtract).then_inc(sem("rope_v"), 1)
                lowpart(i, s, 1, "tr_q2", "q", z.qhl[:, 1], full("tr_q2"), z.qhl[:, 0], 0.25)
                lowpart(i, s, 1, "tr_k2", "k", z.khl[0:64, 1, 0], gbank(s, "tr_k2")[0:64, 0:256],
                        z.khl[0:64, 0, 0], 1.0)
                attention(i, s, 1)
                dve.wait_ge(*written(i, s, "out2"))
                dve.tensor_tensor(z.y[:], z.y[:], full("out2"), ALU.add).then_inc(read_sem(s, "out2"), 1)
                stats(i, s, 3, z.y, read(i, s, "out2"))
                dve.wait_ge(sem(f"res_saved{s}"), 16 * i)
                dve.tensor_tensor(z.res[:], z.y[:], z.h0[:], ALU.add).then_inc(sem("res"), 1)
                dve.tensor_tensor(z.vb[:], z.st[:, :, 0], z.st[:, :, 0], ALU.mult).then_inc(*made(s, "ms"))
                dve.wait_ge(*own(i, s, "ms"))
                dve.scalar_tensor_tensor(out=z.va[:], in0=z.vb[:], scalar=EPS, in1=z.st[:, :, 1], op0=ALU.add,
                                         op1=ALU.add).then_inc(sem("va3"), 1)
                dve.wait_ge(sem("rr3"), i * 2 + s + 1)
                dve.wait_ge(sem(f"scat{s}"), 64 * i)
                for t in range(NT):
                    ins = dve.tensor_scalar(z.xn[:, t], z.y[:, t], z.rr[:, t:t + 1], None, ALU.mult)
                ins.then_inc(sem("xn"), 1)
                dve.wait_ge(*written(i, s, "lgt"))
                dve.tensor_copy(z.lg[:], gbank(s, "lgt")[:, 0:NT * NE].rearrange("p (t e) -> p t e", t=NT))\
                    .then_inc(read_sem(s, "lgt"), 1)
                wait_apart(dve, *read(i, s, "lgt"), 0)
                for t in range(NT):
                    ins = dve.max(z.top[:, t], z.lg[:, t])
                ins.then_inc(*made(s, "top"))
                dve.wait_ge(*own(i, s, "top"))
                dve.tensor_tensor(z.ew[:, :, 0], z.top[:, :, 1], z.top[:, :, 0], ALU.subtract)\
                    .then_inc(sem("dtop"), 1)
                for t in range(NT):
                    ins = dve.max_index(z.idx[:, t], z.top[:, t], z.lg[:, t])
                ins.then_inc(*made(s, "idx"))
                dve.wait_ge(*own(i, s, "idx"))
                dve.tensor_copy(z.ro[:, :, 0:2], z.idx[:, :, 0:2]).then_inc(*made(s, "ro_e"))
                dve.wait_ge(*own(i, s, "ro_e"))
                for t in range(NT):
                    for k in range(2):
                        ins = dve.tensor_scalar(z.oh[:, t, k], small[:, 0:8], z.ro[:, t, k:k + 1], None, ALU.is_equal)
                ins.then_inc(*made(s, "oh"))
                dve.wait_ge(*own(i, s, "oh"))
                dve.tensor_tensor(z.pick[:], z.oh[:, :, 0], z.oh[:, :, 1], ALU.add).then_inc(sem("pick"), 1)
                dve.wait_ge(sem("etop"), i * 2 + s + 1)
                dve.tensor_scalar(z.ew[:, :, 1], z.ew[:, :, 0], 1.0, None, ALU.add).then_inc(*made(s, "wd"))
                dve.wait_ge(*own(i, s, "wd"))
                dve.reciprocal(z.ro[:, :, 4], z.ew[:, :, 1]).then_inc(*made(s, "w0"))
                dve.wait_ge(*own(i, s, "w0"))
                dve.tensor_tensor(z.ro[:, :, 5], z.ew[:, :, 0], z.ro[:, :, 4], ALU.mult).then_inc(*made(s, "w1"))
                dve.wait_ge(*written(i, s, "rank"))
                gb = gbank(s, "rank")
                dve.tensor_tensor(z.rk[:], gb[:, 0:2 * NE].rearrange("p (t e) -> p t e", t=NT),
                                  counts[:].unsqueeze(1).broadcast_to([P, NT, NE]), ALU.add)\
                    .then_inc(*made(s, "rk"))
                dve.wait_ge(*own(i, s, "rk"))
                dve.tensor_tensor(counts[:], counts[:], gb[:, 2 * NE:3 * NE], ALU.add).then_inc(read_sem(s, "rank"), 1)
                dve.tensor_tensor(z.rsel[:], z.oh[:], z.rk[:].unsqueeze(2).broadcast_to([P, NT, 2, NE]), ALU.mult)\
                    .then_inc(*made(s, "rsel"))
                dve.wait_ge(*own(i, s, "rsel"))
                dve.tensor_reduce(z.ro[:, :, 2:4], z.rsel[:], AX.X, ALU.add).then_inc(*made(s, "ro_r"))
                dve.wait_ge(*own(i, s, "ro_r"))
                dve.wait_ge(*read(i, s, "rank"))
                dve.wait_ge(*own(i, s, "w1"))
                dve.scalar_tensor_tensor(out=z.posf[:], in0=z.ro[:, :, 0:2], scalar=float(REGION), in1=z.ro[:, :, 2:4],
                                         op0=ALU.mult, op1=ALU.add).then_inc(*made(s, "posf"))
                dve.tensor_copy(route[:, bass.ds((i * 2 + s) * NT, NT), :], z.ro[:]).then_inc(sem("routed"), 1)
                dve.wait_ge(*own(i, s, "posf"))
                dve.tensor_copy(z.pos[:], z.posf[:]).then_inc(sem("pos"), 1)

            with dve.Fori(0, ITERS) as i:
                for s in range(2):
                    batch(i, s)
            assert len(place) == own_count, len(place)

            for s in range(2):
                dve.wait_ge(sem("routed"), B)
                dve.wait_ge(sem(f"scat{s}"), 64 * ITERS)
                dve.wait_ge(sem(f"res_saved{s}"), 16 * ITERS)
            link(dve.tensor_tensor(gt[:], counts[:].unsqueeze(2).broadcast_to([P, NE, 33]),
                                   small[:, 8:41].unsqueeze(1).broadcast_to([P, NE, 33]), ALU.is_gt))
            link(dve.tensor_reduce(nt[:], gt[:], AX.X, ALU.add))
            link(dve.memset(start[:], 0.0))
            link(dve.memset(zrow[:], 0.0))
            for e in range(1, NE):
                link(dve.tensor_tensor(start[:, e:e + 1], start[:, e - 1:e], nt[:, e - 1:e], ALU.add))
            link(dve.tensor_tensor(zposf[:, 0], counts[:], small[:, 45:53], ALU.add))
            link(dve.tensor_scalar(zposf[:, 0], zposf[:, 0], small[:, 41:42], None, ALU.add))
            link(dve.tensor_scalar(zposf[:, 1], zposf[:, 0], float(P), None, ALU.add))
            dve.tensor_copy(zpos[:], zposf[:]).then_inc(sem("zpos"), 1)
            link(dve.tensor_tensor(over[:], small[:, 64:64 + MT].unsqueeze(1).broadcast_to([P, NE, MT]),
                                   start[:].unsqueeze(2).broadcast_to([P, NE, MT]), ALU.is_ge))
            link(dve.tensor_reduce(tile_e[:], over[:, 1:NE].rearrange("p e j -> p j e"), AX.X, ALU.add))
            link(dve.tensor_tensor(over[:, 1:NE], over[:, 1:NE],
                                   nt[:, 0:NE - 1].unsqueeze(2).broadcast_to([P, NE - 1, MT]), ALU.mult))
            link(dve.tensor_reduce(tile_s[:], over[:, 1:NE].rearrange("p e j -> p j e"), AX.X, ALU.add))
            link(dve.tensor_tensor(tile_l[:], small[:, 64:64 + MT], tile_s[:], ALU.subtract))
            link(dve.tensor_scalar(cap[:], tile_e[:], -1000.0, 1000.0 * (NE - 1), ALU.mult, ALU.add))
            link(dve.tensor_scalar(cap[:], cap[:], nt[:, NE - 1:NE], None, ALU.add))
            link(dve.tensor_tensor(tile_l[:], tile_l[:], cap[:], ALU.min))
            link(dve.tensor_scalar(tile_l[:], tile_l[:], float(P), None, ALU.mult))
            link(dve.scalar_tensor_tensor(out=tile_l[:], in0=tile_e[:], scalar=float(REGION), in1=tile_l[:],
                                          op0=ALU.mult, op1=ALU.add))
            link(dve.tensor_copy(tile_i[:, 0], tile_e[:]))
            dve.tensor_copy(tile_i[:, 1], tile_l[:]).then_inc(sem("tile_i"), 1)
            link(dve.tensor_tensor(eqs[:].rearrange("p (t k) e -> p t k e", k=2),
                                   route[:, :, 0:2].unsqueeze(3).broadcast_to([P, RT, 2, NE]),
                                   small[:, 0:8].unsqueeze(1).unsqueeze(1).broadcast_to([P, RT, 2, NE]), ALU.is_equal))
            link(dve.tensor_tensor(eqs[:], eqs[:], start[:].unsqueeze(1).broadcast_to([P, RT * 2, NE]), ALU.mult))
            link(dve.tensor_reduce(yposf[:].rearrange("p t k -> p (t k)"), eqs[:], AX.X, ALU.add))
            link(dve.scalar_tensor_tensor(out=yposf[:], in0=yposf[:], scalar=float(P), in1=route[:, :, 2:4],
                                          op0=ALU.mult, op1=ALU.add))
            link(dve.tensor_copy(ypos[:], yposf[:]))
            dve.wait_ge(sem("lnm"), 16)
            dve.wait_ge(sem("w13"), 16 * KT)
            for k in range(KT):
                for e in range(NE):
                    dve.tensor_scalar(w13s[:, k, e], w13s[:, k, e], lnm[:, k:k + 1], None, ALU.mult)\
                        .then_inc(sem("w13_scaled"), 1)

            with dve.Fori(0, MT // 2) as j:
                for n in range(2):
                    dve.wait_ge(sem(f"silu{n}"), j + 1)
                    dve.wait_ge(sem(f"tr_g{n}"), j)
                    dve.tensor_tensor(gu[n][:], sg[n][:], bank[3 + 2 * n][:], ALU.mult).then_inc(sem(f"gu{n}"), 1)
                    dve.wait_ge(sem(f"down{n}"), j + 1)
                    dve.wait_ge(sem(f"ys{n}"), 16 * j)
                    dve.tensor_copy(yo[n][:], bank[7][:, 0:D]).then_inc(sem(f"yo{n}"), 1)

            def combine(s, t, dst, res, tag, count):
                dve.scalar_tensor_tensor(out=dst, in0=fy[s][:, t, 0], scalar=fw[s][:, t, 0:1], in1=res,
                                         op0=ALU.mult, op1=ALU.add).then_inc(sem(tag), 1)
                dve.wait_ge(sem(tag), count)
                return dve.scalar_tensor_tensor(out=dst, in0=fy[s][:, t, 1], scalar=fw[s][:, t, 1:2], in1=dst,
                                                op0=ALU.mult, op1=ALU.add)

            with dve.Fori(0, ITERS) as i:
                for s in range(2):
                    dve.wait_ge(sem(f"fy{s}"), 64 * i)
                    dve.wait_ge(sem(f"fo{s}"), i)
                    dve.tensor_copy(fidx[s][:], ypos[:, bass.ds((i * 2 + s) * NT, NT), :]).then_inc(sem(f"fidx{s}"), 1)
                    dve.tensor_copy(fw[s][:], route[:, bass.ds((i * 2 + s) * NT, NT), 4:6]).then_inc(sem(f"fw{s}"), 1)
                for s in range(2):
                    dve.wait_ge(sem(f"fw{s}"), i + 1)
                    dve.wait_ge(sem(f"fy{s}"), 64 * (i + 1))
                    dve.wait_ge(sem(f"fr{s}"), 16 * (i + 1))
                    dve.wait_ge(sem(f"stored{s}"), 32 * i)
                    for t in range(NT):
                        ins = combine(s, t, fo[s][:, t], fr[s][:, t], f"half{s}", i * 2 + t + 1)
                    ins.then_inc(sem(f"fo{s}"), 1)
            dve.tensor_copy(fidx[0][:, 0], ypos[0:P, RT - 1]).then_inc(sem("cls_fi"), 1)
            dve.tensor_copy(fw[0][:, 0], route[:, RT - 1, 4:6]).then_inc(sem("cls_fw"), 1)
            dve.wait_ge(sem("cls_fi"), 1)
            dve.wait_ge(sem("cls_fw"), 1)
            dve.tensor_copy(fw[1][:, 0], route[:, RT - 1, 4:6]).then_inc(sem("cls_fidx"), 1)
            dve.wait_ge(sem("cls_fy"), 32)
            dve.wait_ge(sem("stored0"), 32 * ITERS)
            combine(0, 0, fo[0][:, 0], cls_res[:], "cls_half", 1).then_inc(sem("cls_out"), 1)


def kernel(**inputs):
    import concourse.bacc as _bacc
    from concourse import mybir as _mybir
    from concourse.bass_utils import run_bass_kernel_spmd as _run

    g = {k: np.asarray(v) for k, v in inputs.items()}

    def rows(a, k):
        return np.ascontiguousarray(a.reshape(k, P, -1).transpose(1, 0, 2))

    arrays = {
        "x": g["x"], "cls_tok": g["cls_tok"], "scharr": g["L0_tok_scharr"],
        "wqkv1": rows(g["L0_attn_W_qkv"], KT), "wout1": rows(g["L0_attn_W_out"], KT),
        "ln1": np.ascontiguousarray(g["L0_ffn_ln1_w"].reshape(KT, P).T),
        "ln2": np.ascontiguousarray(g["L0_ffn_ln2_w"].reshape(KT, P).T),
        "wqkv2": rows(g["L0_ffn_wqkv"].T, KT), "wo2": rows(g["L0_ffn_wo"].T, KT),
        "gate": rows(g["L0_ffn_gate_w"].T, KT),
        "w13": np.ascontiguousarray(g["L0_ffn_w13"].transpose(2, 0, 1).reshape(KT, P, NE, 2 * FFN).transpose(1, 0, 2, 3)),
        "w2": np.ascontiguousarray(g["L0_ffn_w2"].transpose(2, 0, 1).reshape(FT, P, NE, D).transpose(1, 0, 2, 3)),
    }
    arrays.update(constants())
    nc = _bacc.Bacc("TRN2", target_bir_lowering=False, num_devices=1)
    in_map, args = {}, []
    for name, a in arrays.items():
        a = np.ascontiguousarray(a)
        in_map[f"in_{name}"] = a
        args.append(nc.dram_tensor(f"in_{name}", a.shape, _mybir.dt.from_np(a.dtype), kind="ExternalInput").ap())
    args.append(nc.dram_tensor("out_0", (B, HW + 1, D), _mybir.dt.float32, kind="ExternalOutput").ap())
    vit_tower(nc, *args)
    r = _run(nc, [in_map], core_ids=[0])
    return r.results[0]["out_0"]
```

```python
from contextlib import ExitStack

import numpy as np

import concourse.bass as bass
from concourse import mybir

P = 128
ALU = mybir.AluOpType
ACT = mybir.ActivationFunctionType
AX = mybir.AxisListType
F32 = mybir.dt.float32
F32R = mybir.dt.float32r
BF16 = mybir.dt.bfloat16
I32 = mybir.dt.int32
U32 = mybir.dt.uint32

B, C3, HW = 16, 3, 256
D = 256
NT = HW // P
KT = D // P
NH, HD = 16, 16
NKV = 4
NE, FFN = 8, 512
FT = FFN // P
GRAY = (0.2989, 0.587, 0.114)
EPS = 1e-5
PAIRS = NH // 2
QC = P + 2
SC = QC + 2 * P + 2
KC = 2 * P + 2
TC = 3 * P
TOKENS = B * HW + 1
REGION = -(-(TOKENS + 2 * P) // P) * P
SLOTS = 2 * TOKENS
MT = -(-(SLOTS + NE * (P - 1)) // P)
MT += MT % 2
GAP = 256
EPAIRS = (MT - 4) // 2
DUMP = NE * REGION
ITERS = B // 2
KV_HEADS = (NH, NKV)
K_TILES = (2, 1)
FIRST_OWN, BODY_OWN = 9, 54
RT = B * NT + 1


def constants():
    k = np.arange(P)[:, None]
    m = np.arange(P)[None, :]
    shifts = np.stack([(k == m + dy - 1) for dy in range(3)], 1).astype(np.float32)
    ident = np.eye(P, dtype=np.float32)
    neg = np.float32(-1e30)
    q0, q1 = k, k + P
    s0, s1 = m, m + P
    cls = np.ones((P, 2), bool)

    def grow(ok):
        return np.where(ok, np.float32(0), neg)

    win = [lambda q, s: (s <= q) & (q - s < 128), lambda q, s: s <= q]
    ms, mt = [], []
    for a in range(2):
        see = win[a]
        c0 = cls & ((q0 + 1 < 128) if a == 0 else True)
        c1 = cls & (a == 1)
        ms.append(grow(np.concatenate([c0, see(q0, s0), c1, see(q1, s0), see(q1, s1)], 1)))
        mt.append(grow(np.concatenate([see(m, k), see(m + P, k), see(m + P, k + P)], 1)))
    mask_s = np.stack(ms, 1)
    mask_t = np.stack(mt, 1)
    inv = (np.float32(1.0) / np.float32(10000.0) ** (np.arange(0, HD, 2, dtype=np.float32) / np.float32(HD)))
    pos = (np.arange(NT, dtype=np.float32)[None, :] * P + np.arange(P, dtype=np.float32)[:, None] + 1)
    ang = (pos[:, :, None] * inv[None, None, :]).astype(np.float32)
    rope = np.stack([np.cos(ang), np.sin(ang)], 1).astype(np.float32)
    prefix = np.concatenate([(k < m), np.ones((P, P))], 1).astype(np.float32)
    small = np.zeros((P, 256), np.float32)
    small[:, 0:8] = np.arange(8)
    small[:, 8:41] = np.arange(33) * P
    small[:, 41] = np.arange(P)
    small[:, 42] = np.arange(P) == 0
    small[:, 43:45] = np.where(np.arange(P)[:, None] == 0, 0, DUMP + np.arange(P)[:, None] + P * np.arange(2))
    small[:, 45:53] = np.arange(8) * REGION
    small[:, 53:55] = -0.5
    small[:, 64:64 + MT] = np.arange(MT)
    return {"c_shift": shifts, "c_ident": ident, "c_masks": mask_s, "c_maskt": mask_t,
            "c_rope": rope, "c_prefix": prefix, "c_small": small}


def vit_tower(nc, x, cls_tok, scharr, wqkv1, wout1, ln1, ln2, wqkv2, wo2, gate, w13, w2,
              c_shift, c_ident, c_masks, c_maskt, c_rope, c_prefix, c_small, out):
    hs = nc.dram_tensor("hs", [DUMP + 2 * P, D], F32, kind="Internal").ap()
    ys = nc.dram_tensor("ys", [MT * P, D], F32, kind="Internal").ap()
    rs = nc.dram_tensor("rs", [B, P, NT * D], F32, kind="Internal").ap()

    qd = [nc.dram_tensor(f"qd{s}", [2, 2, P, 2 * P], F32, kind="Internal").ap() for s in range(2)]
    kd = [nc.dram_tensor(f"kd{s}", [2, 2, P, 2 * P], F32, kind="Internal").ap() for s in range(2)]

    sems = {}
    root = ExitStack()

    def sem(name):
        if name not in sems:
            sems[name] = root.enter_context(nc.semaphore(name))
        return sems[name]

    def sb(ctx, name, shape, dt=F32):
        return ctx.enter_context(nc.sbuf_tensor(name, shape, dt))

    with root:
        small = sb(root, "small", [P, 256])
        ident = sb(root, "ident", [P, P])
        idle = sb(root, "idle", [P, 4])
        route = sb(root, "route", [P, RT, 6])
        counts = sb(root, "counts", [P, NE])
        credit = sb(root, "credit", [P, 16])
        cls_res = sb(root, "cls_res", [P, D])
        unit = [root.enter_context(nc.psum_tensor(f"unit{n}", [P, 2, 512], F32)) for n in range(2)]
        bank = [unit[n // 2][:, n % 2] for n in range(4)]
        bank += [root.enter_context(nc.psum_tensor(f"bank{n}", [P, 512], F32))[:] for n in range(4, 8)]

        A = ExitStack()
        shift = sb(A, "shift", [P, 3, P])
        prefix = sb(A, "prefix", [P, 2, P], BF16)
        identb = sb(A, "identb", [P, P], BF16)
        mask_s = sb(A, "mask_s", [P, 2, SC], BF16)
        mask_t = sb(A, "mask_t", [P, 2, TC], BF16)
        rope = sb(A, "rope", [P, 2, NT, 8])
        taps = sb(A, "taps", [P, 2, 3, 3])
        band = sb(A, "band", [P, 2, 3, P])
        edgew = sb(A, "edgew", [6, 2, P])
        lnw = sb(A, "lnw", [P, 2, KT])
        w_qkv1 = sb(A, "w_qkv1", [P, KT, 3 * D])
        w_out1 = sb(A, "w_out1", [P, KT, D])
        w_qkv2 = sb(A, "w_qkv2", [P, KT, 384])
        w_out2 = sb(A, "w_out2", [P, KT, D])
        w_gate = sb(A, "w_gate", [P, KT, NE])
        vc = [sb(A, f"vc{a}", [P, NH, HD + 1]) for a in range(2)]
        prob = [sb(A, f"prob{n}", [P, 2, TC]) for n in range(2)]
        stage = sb(A, "stage", [P, 1024])

        class Slot:
            pass

        slots = []
        for s in range(2):
            z = Slot()
            slots.append(z)
            z.s = s
            z.xin = sb(A, f"xin{s}", [P, NT, C3, HW])
            z.gray = sb(A, f"gray{s}", [P, NT, HW + 2])
            z.halo = sb(A, f"halo{s}", [6, NT, HW])
            z.h0 = sb(A, f"h0{s}", [P, NT, D])
            z.tmp = sb(A, f"tmp{s}", [P, NT, D])
            z.y = sb(A, f"y{s}", [P, NT, D])
            z.hn = sb(A, f"hn{s}", [P, NT, D])
            z.yT = sb(A, f"yT{s}", [P, KT, 2 * P])
            z.xn = z.hn
            z.res = sb(A, f"res{s}", [P, NT, D])
            z.qhl = sb(A, f"qhl{s}", [P, 2, 2, 2 * P], F32R)
            z.khl = sb(A, f"khl{s}", [P, 2, 2, 2 * P], F32R)
            z.v = [sb(A, f"v1{s}", [P, NT, NH, HD + 1]), sb(A, f"v2{s}", [P, NT, NKV, HD + 1])]
            z.qkv = sb(A, f"qkv{s}", [P, NT, 24, HD])
            z.rot = sb(A, f"rot{s}", [P, NT, 20, HD])
            z.ra = sb(A, f"ra{s}", [P, 4, NT * 20 * 8])
            z.osum = sb(A, f"osum{s}", [P, NT, NH, HD + 1])
            z.ocls = z.osum
            z.rden = sb(A, f"rden{s}", [P, NT, NH])
            z.mx = sb(A, f"mx{s}", [P, NT, NH])
            z.scls = sb(A, f"scls{s}", [P, NT, NH])
            z.pcls = sb(A, f"pcls{s}", [P, NT, NH])
            z.nm = sb(A, f"nm{s}", [P, NT, 2, NH], F32R)
            z.mT = sb(A, f"mT{s}", [32, 2 * P])
            z.bn = sb(A, f"bn{s}", [P, NT, 6])
            z.st = sb(A, f"st{s}", [P, NT, 2])
            z.va = sb(A, f"va{s}", [P, NT])
            z.vb = sb(A, f"vb{s}", [P, NT])
            z.rstd = sb(A, f"rstd{s}", [P, NT])
            z.rr = sb(A, f"rr{s}", [P, NT])
            z.lg = sb(A, f"lg{s}", [P, NT, NE])
            z.top = sb(A, f"top{s}", [P, NT, 8])
            z.idx = sb(A, f"idx{s}", [P, NT, 8], U32)
            z.oh = sb(A, f"oh{s}", [P, NT, 2, NE])
            z.pick = sb(A, f"pick{s}", [P, NT, NE], BF16)
            z.rk = sb(A, f"rk{s}", [P, NT, NE])
            z.rsel = sb(A, f"rsel{s}", [P, NT, 2, NE])
            z.ro = sb(A, f"ro{s}", [P, NT, 6])
            z.ew = sb(A, f"ew{s}", [P, NT, 2])
            z.posf = sb(A, f"posf{s}", [P, NT, 2])
            z.pos = sb(A, f"pos{s}", [P, NT, 2], I32)
            z.qst = sb(A, f"qst{s}", [P, NH, 2 * P], F32R)
            z.kst = [sb(A, f"kst0{s}", [P, NH, KC], F32R), sb(A, f"kst1{s}", [P, NKV, KC], F32R)]
        A.close()

        M = ExitStack()
        lnm = sb(M, "lnm", [P, KT])
        nt = sb(M, "nt", [P, NE])
        gt = sb(M, "gt", [P, NE, 33])
        start = sb(M, "start", [P, NE])
        over = sb(M, "over", [P, NE, MT])
        tile_e = sb(M, "tile_e", [P, MT])
        tile_s = sb(M, "tile_s", [P, MT])
        tile_l = sb(M, "tile_l", [P, MT])
        cap = sb(M, "cap", [P, MT])
        tile_i = sb(M, "tile_i", [P, 2, MT], I32)
        zrow = sb(M, "zrow", [P, D])
        zposf = sb(M, "zposf", [P, 2, NE])
        zpos = sb(M, "zpos", [P, 2, NE], I32)
        eqs = sb(M, "eqs", [P, RT * 2, NE])
        yposf = sb(M, "yposf", [P, RT, 2])
        ypos = sb(M, "ypos", [P, RT, 2], I32)
        xt = [sb(M, f"xt{n}", [P, D]) for n in range(2)]
        xT = [sb(M, f"xT{n}", [P, 2, KT * P], F32R) for n in range(2)]
        sg = [sb(M, f"sg{n}", [P, FFN]) for n in range(2)]
        gu = sg
        guT = [sb(M, f"guT{n}", [P, FT, P]) for n in range(2)]
        yo = [sb(M, f"yo{n}", [P, D]) for n in range(2)]
        fr = [sb(M, f"fr{n}", [P, NT, D]) for n in range(2)]
        fy = [sb(M, f"fy{n}", [P, NT, 2, D]) for n in range(2)]
        fw = [sb(M, f"fw{n}", [P, NT, 2]) for n in range(2)]
        fidx = [sb(M, f"fidx{n}", [P, NT, 2], I32) for n in range(2)]
        fo = [sb(M, f"fo{n}", [P, NT, D]) for n in range(2)]
        sb(M, "gap", [P, GAP])
        w13l = sb(M, "w13l", [P, KT, NE, 2 * FFN], F32R)
        w13h = sb(M, "w13h", [P, KT, NE, 2 * FFN], F32R)
        w2s = sb(M, "w2s", [P, FT, NE, D])
        M.close()

        block = root.enter_context(nc.Block())

        FRONT = ["gray", "conv", "sum1", "norm1", "tr_y1", "v1", "qk1"]
        ATTEND = [[f"s{n}{a}" for n in range(PAIRS)] + [f"mt{a}"] + [f"st{n}{a}" for n in range(PAIRS)] + [f"pv{a}"]
                  for a in range(2)]
        MIDDLE_0 = {1: ["o1"], 3: ["tr_o1"], 4: ["out1"], 5: ["norm2"], 6: ["hn"], 7: ["tr_y2"], 8: ["qkv2"],
                    9: ["rope"], 10: ["qk2"]}
        MIDDLE_1 = {1: ["o1"], 3: ["tr_o1"], 4: ["out1"], 5: ["norm2"], 6: ["hn"], 7: ["tr_y2"],
                    8: ["qkv2", "rope"], 10: ["qk2"]}
        BACK_0 = {0: ["o2"], 1: ["tr_o2"], 4: ["out2"], 5: ["xn"], 7: ["tr_x", "lgt"], 11: ["rank"],
                  12: ["scatter"]}
        FRONT_0 = {2: ["gray"], 5: ["conv"], 6: ["sum1"], 7: ["norm1"], 8: ["tr_y1"], 10: ["v1", "qk1"]}
        BACK_1 = {0: ["o2"], 1: ["tr_o2"], 4: ["out2"], 5: ["xn"], 6: ["tr_x"], 7: ["lgt"], 11: ["rank"],
                  12: ["scatter"]}
        FRONT_1 = {2: ["gray"], 5: ["conv"], 6: ["sum1"], 7: ["norm1"], 8: ["tr_y1"], 9: ["v1"], 11: ["qk1"]}
        LOAD_NEXT = {12: ["load"]}
        for steps in (FRONT_0, FRONT_1):
            assert sorted(sum(steps.values(), [])) == sorted(FRONT)

        def run(ahead, s, a, others):
            mixed = []
            for n, stage in enumerate(ATTEND[a]):
                mixed.append((ahead, s, stage))
                for turns, steps in others:
                    mixed += [(turns, 1 - s, x) for x in steps.get(n, [])]
            return mixed

        BODY = (run(0, 1, 0, [(0, MIDDLE_0), (1, LOAD_NEXT)])
                + run(0, 0, 1, [(0, MIDDLE_1), (1, LOAD_NEXT)])
                + run(0, 1, 1, [(0, BACK_0), (1, FRONT_0)])
                + run(1, 0, 0, [(0, BACK_1), (1, FRONT_1)]))
        FIRST = [(1, 0, x) for x in FRONT] + run(1, 0, 0, [(1, FRONT_1)])
        LAST = [x for x in BODY if x[0] == 0]
        USES = {"conv": ["conv0", "conv1"], "tr_y1": ["tr_y1"], "qk1": ["q1", "k1"], "v1": ["v1"],
                "mt0": ["mt1"], "tr_o1": ["tr_o1"], "out1": ["out1"], "tr_y2": ["tr_y2"],
                "qkv2": ["qkv2a", "qkv2b"], "qk2": ["tr_q2", "tr_k2"], "mt1": ["mt2"], "tr_o2": ["tr_o2"],
                "out2": ["out2"], "tr_x": ["tr_x"], "lgt": ["lgt"], "rank": ["rank"]}

        class Part:

            def __init__(self, order, uses_before, own_before, turns):
                self.order = order
                self.uses = [(s, g) for _, s, stage in order for g in USES.get(stage, [])]
                self.uses_before, self.own_before = uses_before, own_before
                self.turns, self.place, self.i = turns, {}, 0

        first = Part(FIRST, 0, 0, 1)
        body = Part(BODY, len(first.uses), FIRST_OWN, ITERS - 1)
        last = Part(LAST, body.uses_before + body.turns * len(body.uses),
                    body.own_before + body.turns * BODY_OWN, 1)
        assert len(body.uses) % 2 == 0
        at = [first]

        def go_through(eng, stages):
            def steps(part, i):
                at[0] = part
                for ahead, s, stage in part.order:
                    if stage in stages:
                        stages[stage](i + ahead if ahead else i, s)

            steps(first, -1)
            with eng.Fori(0, ITERS - 1) as i:
                body.i = i
                steps(body, i)
            steps(last, ITERS - 1)

        def turn(n):
            return n * body.i if at[0] is body else 0

        def use_before(s, g):
            return at[0].uses_before + at[0].uses.index((s, g))

        def gbank(s, g):
            return bank[6 + use_before(s, g) % 2]

        def order_of(i, s, a):
            return i * 4 + 2 * a + s

        def wait_apart(eng, which, value, col):
            eng.wait_ge(which, value)
            return eng.tensor_tensor(idle[:, col:col + 1], small[:, 0:1], small[:, 0:1], ALU.add)

        def tile(t):
            return slice(t, t + 1) if isinstance(t, int) else bass.ds(t, 1)

        def wait_met(eng, which, value):
            if not (isinstance(value, int) and value <= 0):
                eng.wait_ge(which, value)

        def written(i, s, g):
            return sem("g_written"), turn(len(body.uses)) + use_before(s, g) + 1

        def read_sem(s, g):
            return sem(f"bank{6 + use_before(s, g) % 2}_read")

        def read(i, s, g):
            return read_sem(s, g), turn(len(body.uses) // 2) + use_before(s, g) // 2 + 1

        def g_free(pe, i, s, g):
            wait_met(pe, read_sem(s, g), turn(len(body.uses) // 2) + use_before(s, g) // 2)

        CLS = ["load", "start", "bn", "aggr", "var", "pow", "ln", "tr", "trc", "qkv", "kh", "kl", "vcopy",
               "kdma", "tro", "troc", "out", "res",
               "bn2", "aggr2", "var2", "pow2", "va2", "vb2", "pow2b", "y2", "hn2", "tr2", "tr2c", "qkv2", "qkv2c",
               "trk", "kh2", "kl2", "vcopy2", "kdma2", "tro2", "troc2", "out2", "x2", "res2",
               "bn3", "aggr3", "sq3", "var3", "pow3", "xn3", "tr3", "tr3c", "lgt", "lgtc",
               "max", "midx", "midf", "dif", "exp", "den", "w0", "w1", "oh0", "oh1", "cnt", "rank0", "pose", "posm",
               "posd", "posi", "scat"]

        def after(eng, name):
            eng.wait_ge(sem("cls"), CLS.index(name) + 1)

        Z = slots[0]

        @block.sync
        def _(sp):
            n_const = 0
            for dst, src in ((small[:], c_small), (ident[:], c_ident), (shift[:], c_shift), (rope[:], c_rope),
                             (w_qkv1[:], wqkv1), (w_out1[:], wout1), (w_qkv2[:], wqkv2), (w_out2[:], wo2),
                             (w_gate[:], gate), (lnw[:, 0], ln1), (lnw[:, 1], ln2),
                             (stage[:, 0:2 * SC], c_masks.rearrange("p a c -> p (a c)")),
                             (taps[:], scharr.rearrange("f o y x -> o (f y x)").partition_broadcast(P)
                              .rearrange("p o (f y x) -> p (o f) y x", f=2, y=3)),
                             (Z.h0[:, 0], cls_tok[0, 0:1, :].partition_broadcast(P).rearrange("p o d -> p (o d)"))):
                sp.dma_start(dst, src).then_inc(sem("const"), 16)
                n_const += 16
            sp.wait_ge(sem("edgew_clear"), 1)
            for f in range(2):
                for side in range(2):
                    dst = edgew[3 * side:3 * side + 3, f, (P - 1) * side:(P - 1) * side + 1]
                    sp.dma_start(dst, scharr[f, 0, 2 * side, :].unsqueeze(1)).then_inc(sem("edgew"), 16)
            sp.wait_ge(sem("mask_s_cast"), 1)
            sp.dma_start(stage[:, 0:2 * TC], c_maskt.rearrange("p a c -> p (a c)")).then_inc(sem("stage2"), 16)
            sp.wait_ge(sem("mask_t_cast"), 1)
            sp.dma_start(stage[:, 0:2 * P], c_prefix).then_inc(sem("stage3"), 16)

            def load(i, s):
                z = slots[s]
                wait_met(sp, sem("gray"), i * 2 + s - 1)
                for t in range(NT):
                    src = x[bass.ds(i * 2 + s, 1), :, t * P:(t + 1) * P, :].rearrange("o c p w -> p (o c) w")
                    sp.dma_start(z.xin[:, t], src).then_inc(sem(f"xin{s}"), 16)

            for s in range(2):
                load(0, s)

            for a in range(2):
                after(sp, ("kl", "kl2")[a])
                rows = KV_HEADS[a] * HD // K_TILES[a]
                sp.dma_start(kd[a][:, 0:K_TILES[a], 0:rows, 0:2].rearrange("a m p q -> p a m q"),
                             Z.khl[0:rows, :, 0:K_TILES[a], 0:2].bitcast(F32)).then_inc(sem("kcls_out"), 16)
                sp.wait_ge(sem("kcls_out"), 16 * (a + 1))
                for z in slots:
                    for part, row in ((0, 0), (1, 16), (0, 32), (1, 48)):
                        src = kd[a][part].rearrange("m (h d) q -> d (m h) q", d=HD)[:, 0:KV_HEADS[a], 0:2]
                        sp.dma_start(z.kst[a][row:row + 16, :, 0:2].bitcast(F32), src).then_inc(sem("kcls"), 16)

            def halo(i, s):
                z = slots[s]
                sp.wait_ge(sem("gray"), i * 2 + s + 1)
                for dx in range(3):
                    sp.dma_start(z.halo[dx:dx + 1, 1], z.gray[P - 1:P, 0, dx:dx + HW]).then_inc(sem(f"halo{s}"), 16)
                    sp.dma_start(z.halo[3 + dx:4 + dx, 0], z.gray[0:1, 1, dx:dx + HW]).then_inc(sem(f"halo{s}"), 16)

            def stack(i, s, a):
                z = slots[s]
                sp.wait_ge(*read(i, s, ("q1", "tr_q2")[a]))
                sp.dma_start(qd[s].rearrange("a m p q -> p (a m) q"),
                             z.qhl[:].rearrange("p a m q -> p (a m) q").bitcast(F32)).then_inc(sem(f"qd{s}"), 16)
                sp.wait_ge(*read(i, s, ("k1", "tr_k2")[a]))
                rows = KV_HEADS[a] * HD // K_TILES[a]
                sp.dma_start(kd[s][:, 0:K_TILES[a], 0:rows].rearrange("a m p q -> p a m q"),
                             z.khl[0:rows, :, 0:K_TILES[a]].bitcast(F32)).then_inc(sem(f"kd{s}"), 16)
                sp.wait_ge(sem(f"qd{s}"), 16 * (2 * i + a + 1))
                sp.dma_start(z.qst[64:66].bitcast(F32), z.qst[66:68].bitcast(F32)).then_inc(sem(f"qst{a}{s}"), 16)
                for part, row in ((0, 0), (0, 16), (1, 32), (1, 48)):
                    sp.dma_start(z.qst[row:row + 16].bitcast(F32),
                                 qd[s][part].rearrange("m (h d) q -> d (m h) q", d=HD)).then_inc(sem(f"qst{a}{s}"), 16)
                sp.wait_ge(sem(f"kd{s}"), 16 * (2 * i + a + 1))
                for part, row in ((0, 0), (1, 16), (0, 32), (1, 48)):
                    src = kd[s][part].rearrange("m (h d) q -> d (m h) q", d=HD)[:, 0:KV_HEADS[a]]
                    sp.dma_start(z.kst[a][row:row + 16, :, 2:KC].bitcast(F32), src).then_inc(sem(f"kst{a}{s}"), 16)

            def maxrows(i, s, a):
                z = slots[s]
                sp.wait_ge(*read(i, s, f"mt{a + 1}"))
                for part in range(2):
                    sp.dma_start(z.qst[64 + part:65 + part].bitcast(F32), z.mT[part * NH:(part + 1) * NH])\
                        .then_inc(sem(f"mrow{a}{s}"), 16)

            def residual(i, s):
                z = slots[s]
                sp.wait_ge(sem("res"), i * 2 + s + 1)
                sp.dma_start(rs[bass.ds(i * 2 + s, 1)].rearrange("o p d -> p (o d)"),
                             z.res[:].rearrange("p t d -> p (t d)")).then_inc(sem(f"res_saved{s}"), 16)

            def gate_up_weights(i, s):
                if at[0] is last and s == 0:
                    sp.wait_ge(sem("scat0"), 64 * ITERS + 16)
                    sp.wait_ge(sem("res_saved0"), 16 * ITERS + 1)
                    sp.wait_ge(sem("routed"), B - 1)
                    for e in range(0, NE, 2):
                        sp.dma_start(w13l[:, :, e:e + 2].bitcast(F32), w13[:, :, e:e + 2])\
                            .then_inc(sem(f"w13_{e}"), 16)

            go_through(sp, {"scatter": gate_up_weights, "load": load, "gray": halo, "qk1": lambda i, s: stack(i, s, 0),
                            "mt0": lambda i, s: maxrows(i, s, 0), "qk2": lambda i, s: stack(i, s, 1),
                            "mt1": lambda i, s: maxrows(i, s, 1), "xn": residual})

            for s in range(2):
                sp.wait_ge(sem(f"scat{s}"), 64 * ITERS + 16)
                sp.wait_ge(sem(f"res_saved{s}"), 16 * ITERS + 1)
                sp.wait_ge(sem("routed"), B)
            sp.dma_start(lnm[:], ln2).then_inc(sem("lnm"), 16)

            sp.wait_ge(sem("tile_i"), 1)
            sp.wait_ge(sem("zero"), 16 * 2 * NE)
            def tile_in(t, n):
                row = sp.value_load(tile_i[0:1, 1, t], min_val=0, max_val=DUMP - P)
                sp.dma_start(xt[n][:], hs[bass.ds(row, P), :]).then_inc(sem(f"xt{n}"), 16)

            def tile_out(t, n):
                sp.wait_ge(sem("yo"), t + 1)
                sp.dma_start(ys[bass.ds(t * P, P), :], yo[n][:]).then_inc(sem(f"ys{n}"), 16)

            def move(t, n, load=True):
                if load:
                    sp.wait_ge(sem("tr_e"), t + 2)
                    tile_in(tile(t + 3), 1 - n)
                tile_out(t - 1, 1 - n)

            for t in range(2):
                tile_in(tile(t), t)
            sp.dma_start(w2s[:], w2).then_inc(sem("w2"), 16)
            for t in range(2, 4):
                sp.wait_ge(sem("tr_e"), t - 1)
                tile_in(tile(t), t % 2)
            move(1, 1)
            move(2, 0)
            with sp.Fori(0, EPAIRS - 1) as j:
                move(j * 2 + 3, 1)
                move(j * 2 + 4, 0)
            move(MT - 3, 1, load=False)
            move(MT - 2, 0, load=False)
            move(MT - 1, 1, load=False)
            tile_out(MT - 1, 1)
            for n in range(2):
                sp.wait_ge(sem(f"ys{n}"), 16 * (MT // 2))
            sp.dma_start(zrow[0:1, 0:1], small[0:1, 0:1]).then_inc(sem("ys_all"), 16)

            with sp.Fori(0, ITERS) as i:
                for s in range(2):
                    sp.wait_ge(sem(f"fo{s}"), i + 1)
                    sp.dma_start(fr[s][:].rearrange("p t d -> p (t d)"),
                                 rs[bass.ds(i * 2 + s, 1)].rearrange("o p d -> p (o d)")).then_inc(sem(f"fr{s}"), 16)
                for s in range(2):
                    sp.wait_ge(sem(f"fo{s}"), i + 2)
                    for t in range(NT):
                        dst = out[bass.ds(i * 2 + s, 1), 1 + t * P:1 + (t + 1) * P, :].rearrange("o p d -> p (o d)")
                        sp.dma_start(dst, fo[s][:, t]).then_inc(sem(f"stored{s}"), 16)
            sp.wait_ge(sem("cls_out"), 1)
            sp.dma_start(out[:, 0, :], fo[0][0:B, 0]).then_inc(sem("stored0"), 16)
            sp.wait_ge(sem("stored0"), 32 * ITERS + 17)
            sp.wait_ge(sem("stored1"), 32 * ITERS + 1)

        @block.gpsimd
        def _(pool):
            pool.memset(edgew[:], 0.0).then_inc(sem("edgew_clear"), 1)
            for z in slots:
                pool.memset(z.gray[:], 0.0).then_inc(sem("cleared"), 1)
                pool.memset(z.halo[:], 0.0).then_inc(sem("cleared"), 1)
                pool.memset(z.v[0][:], 1.0).then_inc(sem("cleared"), 1)
                pool.memset(z.v[1][:], 1.0).then_inc(sem("cleared"), 1)
            steps = 8
            for z in slots:
                for part, value in ((z.qst[64:P].bitcast(F32), 0.0), (z.kst[0][64:P].bitcast(F32), 0.0),
                                    (z.kst[1][64:P].bitcast(F32), 0.0), (z.kst[0][64:66].bitcast(F32), 1.0),
                                    (z.kst[1][64:66].bitcast(F32), 1.0), (vc[z.s][:], 1.0)):
                    pool.wait_ge(sem("cleared"), steps)
                    pool.memset(part, value).then_inc(sem("cleared"), 1)
                    steps += 1
            for n, name in enumerate(("res_saved0", "res_saved1", "fo0", "fo1",
                                      "stored0", "stored1", "idled0", "idled1")):
                pool.memset(credit[:, n:n + 1], 0.0).then_inc(sem(name), 1)
            pool.wait_ge(sem("const"), 16 * 14)

            def rsqrt(ins, outs, ready, done):
                pool.wait_ge(*ready)
                pool.tensor_tensor(outs, ins, small[:, 53:54].broadcast_to([P, ins.shape[1]]), ALU.pow).then_inc(*done)

            c = sem("cls")
            rsqrt(Z.va[:, 0:1], Z.rstd[:, 0:1], (c, CLS.index("pow")), (c, 1))
            rsqrt(Z.va[:, 0:1], Z.rstd[:, 0:1], (c, CLS.index("pow2")), (c, 1))
            rsqrt(Z.vb[:, 0:1], Z.rr[:, 0:1], (c, CLS.index("pow2b")), (c, 1))
            rsqrt(Z.va[:, 0:1], Z.rr[:, 0:1], (c, CLS.index("pow3")), (c, 1))
            after(pool, "posi")
            for k in range(2):
                pool.indirect_dma_start(out=hs, out_offset=bass.IndirectOffsetOnAxis(ap=Z.pos[:, 0, k:k + 1], axis=0),
                                        in_=Z.xn[:, 0], in_offset=None).then_inc(sem(f"scat{k}"), 16)

            def rope_half(i, s):
                z = slots[s]
                pool.wait_ge(*read(i, s, "qkv2b"))
                x1, x2 = z.qkv[:, :, 0:20, 0:8], z.qkv[:, :, 0:20, 8:16]
                co = rope[:, 0].unsqueeze(2).broadcast_to([P, NT, 20, 8])
                si = rope[:, 1].unsqueeze(2).broadcast_to([P, NT, 20, 8])
                r2 = z.ra[:, 2].rearrange("p (t h d) -> p t h d", t=NT, h=20)
                r3 = z.ra[:, 3].rearrange("p (t h d) -> p t h d", t=NT, h=20)
                pool.tensor_tensor(r2, x2, co, ALU.mult).then_inc(sem("rope_p"), 1)
                pool.tensor_tensor(r3, x1, si, ALU.mult).then_inc(sem("rope_p"), 1)
                pool.wait_ge(sem("rope_p"), (i * 2 + s) * 3 + 2)
                pool.tensor_tensor(z.rot[:, :, :, 8:16], r2, r3, ALU.add).then_inc(sem("rope_p"), 1)
                pool.tensor_copy(z.v[1][:, :, :, 0:HD], z.qkv[:, :, 20:24, :]).then_inc(sem("v2"), 1)

            def class_value(i, s, a):
                z = slots[s]
                pool.wait_ge(sem("pcls"), order_of(i, s, a) + 1)
                for t in range(NT):
                    pool.tensor_tensor(z.ocls[:, t], vc[a][:], z.pcls[:, t].unsqueeze(2).broadcast_to([P, NH, HD + 1]),
                                       ALU.mult).then_inc(sem("ocls"), 1)

            def scatter(i, s):
                z = slots[s]
                wait_apart(pool, sem("pos"), i * 2 + s + 1, 1)
                for t in range(NT):
                    for k in range(2):
                        pool.indirect_dma_start(
                            out=hs, out_offset=bass.IndirectOffsetOnAxis(ap=z.pos[:, t, k:k + 1], axis=0),
                            in_=z.xn[:, t], in_offset=None).then_inc(sem(f"scat{s}"), 16)

            go_through(pool, {
                "sum1": lambda i, s: rsqrt(slots[s].va[:], slots[s].rstd[:], (sem("va1"), i * 2 + s + 1), (sem("rstd1"), 1)),
                "out1": lambda i, s: rsqrt(slots[s].va[:], slots[s].rstd[:], (sem("va2"), i * 2 + s + 1), (sem("rstd2"), 1)),
                "norm2": lambda i, s: rsqrt(slots[s].vb[:], slots[s].rr[:], (sem("vb2"), i * 2 + s + 1), (sem("rr2"), 1)),
                "out2": lambda i, s: rsqrt(slots[s].va[:], slots[s].rr[:], (sem("va3"), i * 2 + s + 1), (sem("rr3"), 1)),
                "mt0": lambda i, s: class_value(i, s, 0), "mt1": lambda i, s: class_value(i, s, 1),
                "rope": rope_half, "scatter": scatter})

            pool.wait_ge(sem("zpos"), 1)
            for e in range(NE):
                for k in range(2):
                    pool.indirect_dma_start(out=hs, out_offset=bass.IndirectOffsetOnAxis(ap=zpos[:, k, e:e + 1], axis=0),
                                            in_=zrow[:], in_offset=None).then_inc(sem("zero"), 16)

            pool.wait_ge(sem("ys_all"), 16)

            def gather(s, t, k, done):
                pool.indirect_dma_start(out=fy[s][:, t, k], out_offset=None, in_=ys,
                                        in_offset=bass.IndirectOffsetOnAxis(ap=fidx[s][:, t, k:k + 1], axis=0))\
                    .then_inc(done, 16)

            with pool.Fori(0, ITERS) as i:
                for s in range(2):
                    pool.wait_ge(sem(f"idled{s}"), i + 1)
                    wait_apart(pool, sem(f"fidx{s}"), i + 1, 2 + s).then_inc(sem(f"idled{s}"), 1)
                    for t in range(NT):
                        for k in range(2):
                            gather(s, t, k, sem(f"fy{s}"))
            pool.wait_ge(sem("cls_fidx"), 1)
            for k in range(2):
                gather(0, 0, k, sem("cls_fy"))

        @block.scalar
        def _(act):
            act.wait_ge(sem("const"), 16 * 14)

            def ccopy(dst, src, name, before):
                after(act, before)
                act.activation(dst, src, ACT.Copy).then_inc(sem("cls"), 1)

            fb = bank[6]
            for (name, before) in (("trc", "tr"), ("troc", "tro"), ("tr2c", "tr2"), ("qkv2c", "qkv2"),
                                   ("troc2", "tro2"), ("tr3c", "tr3")):
                if name == "qkv2c":
                    ccopy(Z.qkv[:, 0], fb[:, 0:384], name, before)
                else:
                    ccopy(Z.yT[:, :, 0:P], fb[:, 0:2 * P], name, before)
            after(act, "dif")
            act.activation(Z.ew[:, 0, 0:1], Z.ew[:, 0, 0:1], ACT.Exp).then_inc(sem("cls"), 1)

            def edges(i, s):
                z = slots[s]
                act.wait_ge(*written(i, s, "conv0"))
                wait_met(act, sem("res"), i * 2 + s - 1)
                act.activation(z.h0[:], gbank(s, "conv0")[:], ACT.Abs, scale=0.5).then_inc(read_sem(s, "conv0"), 1)
                act.wait_ge(*written(i, s, "conv1"))
                act.activation(z.tmp[:], gbank(s, "conv1")[:], ACT.Abs, scale=0.5).then_inc(read_sem(s, "conv1"), 1)

            def take(i, s, g, dst, src, scale=1.0):
                act.wait_ge(*written(i, s, g))
                act.activation(dst, src, ACT.Copy, scale=scale).then_inc(read_sem(s, g), 1)

            def high(i, s, a, g, key, dst, src, scale):
                act.wait_ge(*written(i, s, g))
                act.activation(dst, src, ACT.Copy, scale=scale).then_inc(sem(f"{key}hi{a}"), 1)

            def class_weight(i, s, a):
                z = slots[s]
                take(i, s, f"mt{a + 1}", z.mT[:], gbank(s, f"mt{a + 1}")[0:32, 0:2 * P])
                act.wait_ge(sem("dcls"), order_of(i, s, a) + 1)
                act.activation(z.pcls[:], z.pcls[:], ACT.Exp).then_inc(sem("pcls"), 1)

            def exponentials(i, s, a, p):
                act.wait_ge(sem("st"), order_of(i, s, a) * PAIRS + p + 1)
                wait_met(act, sem("pv"), order_of(i, s, a) * PAIRS + p - 1)
                act.activation(prob[p % 2][:], unit[p % 2][:, :, 0:TC], ACT.Exp).then_inc(sem("exp"), 1)

            def full(s, g):
                return gbank(s, g)[:].rearrange("p (k q) -> p k q", k=2)

            def high1(i, s):
                high(i, s, 0, "q1", "q", slots[s].qhl[:, 0], full(s, "q1"), 0.25)
                high(i, s, 0, "k1", "k", slots[s].khl[:, 0], full(s, "k1"), 1.0)

            def values1(i, s):
                act.wait_ge(*written(i, s, "v1"))
                for t in range(NT):
                    ins = act.activation(slots[s].v[0][:, t, :, 0:HD],
                                         full(s, "v1")[:, t].rearrange("p (h d) -> p h d", h=NH), ACT.Copy)
                ins.then_inc(read_sem(s, "v1"), 1)

            def rows2(i, s):
                for t, g in enumerate(("qkv2a", "qkv2b")):
                    take(i, s, g, slots[s].qkv[:, t].rearrange("p h d -> p (h d)"), gbank(s, g)[:, 0:384])

            def high2(i, s):
                high(i, s, 1, "tr_q2", "q", slots[s].qhl[:, 0], full(s, "tr_q2"), 0.25)
                high(i, s, 1, "tr_k2", "k", slots[s].khl[0:64, 0, 0], gbank(s, "tr_k2")[0:64, 0:256], 1.0)

            def second_share(i, s):
                z = slots[s]
                act.wait_ge(sem("dtop"), i * 2 + s + 1)
                act.activation(z.ew[:, :, 0], z.ew[:, :, 0], ACT.Exp).then_inc(sem("etop"), 1)

            share = {"conv": edges, "qk1": high1, "v1": values1, "qkv2": rows2, "qk2": high2, "lgt": second_share}
            for g in ("tr_y1", "tr_o1", "tr_y2", "tr_o2", "tr_x"):
                share[g] = lambda i, s, g=g: take(i, s, g, slots[s].yT[:], full(s, g))
            for a in range(2):
                share[f"mt{a}"] = lambda i, s, a=a: class_weight(i, s, a)
                for n in range(PAIRS):
                    share[f"st{n}{a}"] = lambda i, s, a=a, n=n: exponentials(i, s, a, n)
            go_through(act, share)

            act.wait_ge(sem("lnm"), 16)
            for e in range(NE):
                act.wait_ge(sem(f"w13_{e // 2 * 2}"), 16)
                for k in range(KT):
                    act.activation(w13h[:, k, e], w13l[:, k, e].bitcast(F32), ACT.Copy, scale=lnm[:, k:k + 1])\
                        .then_inc(sem("w13_high"), 1)

            def expert_copy_in(t, n):
                act.wait_ge(sem("tr_e"), t + 1)
                act.activation(xT[n][:, 0], bank[0][:, 0:2 * P], ACT.Copy).then_inc(sem("xT_high"), 1)

            def expert_hidden_T(t, n):
                act.wait_ge(sem("tr_g"), t + 1)
                act.activation(guT[n][:], bank[6][:], ACT.Copy).then_inc(sem("guT"), 1)

            def expert_silu(t, n):
                act.wait_ge(sem("up"), t + 1)
                act.activation(sg[n][:], bank[2 + 2 * n][:], ACT.Silu).then_inc(sem("silu"), 1)

            def expert_step(t, n, ahead=True):
                expert_hidden_T(t - 1, 1 - n)
                expert_silu(t, n)
                if ahead:
                    expert_copy_in(t + 1, 1 - n)

            expert_copy_in(0, 0)
            expert_silu(0, 0)
            expert_copy_in(1, 1)
            expert_step(1, 1)
            expert_step(2, 0)
            with act.Fori(0, EPAIRS) as j:
                expert_step(j * 2 + 3, 1)
                expert_step(j * 2 + 4, 0)
            expert_step(MT - 1, 1, ahead=False)
            expert_hidden_T(MT - 1, 1)

        @block.tensor
        def _(pe):
            pe.wait_ge(sem("const"), 16 * 14)

            def cmm(name, before, groups):
                after(pe, before)
                for dst, pairs in groups:
                    for n, (lt, rh) in enumerate(pairs):
                        ins = pe.matmul(dst, lt, rh, start=(n == 0), stop=(n == len(pairs) - 1))
                ins.then_inc(sem("cls"), 1)

            def ctr(name, before, src, cols=(P, P)):
                after(pe, before)
                for n, c in enumerate(cols):
                    ins = pe.transpose(fb[0:c, n * P:(n + 1) * P], src[:, n * P:n * P + c], ident[:])
                ins.then_inc(sem("cls"), 1)

            fb, fc, fd = bank[6], bank[7], bank[4]
            fk = [(Z.yT[:, k, 0:P]) for k in range(KT)]
            ctr("tr", "ln", Z.y[:, 0])
            cmm("qkv", "trc",
                [(fc[:, 0:D], [(fk[k], w_qkv1[:, k, 2 * D:3 * D]) for k in range(KT)])]
                + [(fd[:, m * P:(m + 1) * P], [(w_qkv1[:, k, D + m * P:D + (m + 1) * P], fk[k]) for k in range(KT)])
                   for m in range(2)])
            ctr("tro", "kdma", Z.tmp[:, 0])
            cmm("out", "troc", [(fc[:, 0:D], [(fk[k], w_out1[:, k]) for k in range(KT)])])
            ctr("tr2", "hn2", Z.hn[:, 0])
            pe.wait_ge(sem("scaled_w"), 1)
            cmm("qkv2", "tr2c", [(fb[:, 0:384], [(fk[k], w_qkv2[:, k]) for k in range(KT)])])
            after(pe, "qkv2c")
            pe.transpose(fd[0:64, 0:P], Z.qkv[:, 0, 16:20, :].rearrange("p h d -> p (h d)"), ident[:])\
                .then_inc(sem("cls"), 1)
            ctr("tro2", "kdma2", Z.tmp[:, 0])
            cmm("out2", "troc2", [(fc[:, 0:D], [(fk[k], w_out2[:, k]) for k in range(KT)])])
            ctr("tr3", "xn3", Z.xn[:, 0])
            cmm("lgt", "tr3c", [(fc[:, 0:NE], [(fk[k], w_gate[:, k]) for k in range(KT)])])
            after(pe, "scat")
            pe.wait_ge(sem("masks"), 3)
            pe.wait_ge(sem("bands"), 1)
            pe.wait_ge(sem("edgew"), 64)
            pe.wait_ge(sem("kcls"), 16 * 16)
            pe.wait_ge(sem("cleared"), 20)

            def conv(i, s):
                z = slots[s]
                for f in range(2):
                    g_free(pe, i, s, f"conv{f}")
                    if f == 0:
                        pe.wait_ge(sem("gray"), i * 2 + s + 1)
                    for dx in range(3):
                        pe.matmul(gbank(s, f"conv{f}")[:], band[:, f, dx], z.gray[:, :, dx:dx + HW],
                                  start=(dx == 0), stop=False)
                    if f == 0:
                        pe.wait_ge(sem(f"halo{s}"), 16 * 6 * (i + 1))
                    pe.matmul(gbank(s, f"conv{f}")[:], edgew[:, f], z.halo[:], start=False, stop=True)\
                        .then_inc(sem("g_written"), 1)

            def tr(i, s, g, src, ready):
                g_free(pe, i, s, g)
                pe.wait_ge(sem(ready), i * 2 + s + 1)
                for k in range(KT):
                    for t in range(NT):
                        c = k * 2 * P + t * P
                        ins = pe.transpose(gbank(s, g)[:, c:c + P], src[:, t, k * P:(k + 1) * P], ident[:])
                ins.then_inc(sem("g_written"), 1)

            def project_T(i, s, g, w, c0):
                g_free(pe, i, s, g)
                for m in range(2):
                    for k in range(KT):
                        ins = pe.matmul(gbank(s, g)[:, m * 2 * P:(m + 1) * 2 * P],
                                        w[:, k, c0 + m * P:c0 + (m + 1) * P], slots[s].yT[:, k],
                                        start=(k == 0), stop=(k == KT - 1))
                ins.then_inc(sem("g_written"), 1)

            def project(i, s, g, w, c0):
                g_free(pe, i, s, g)
                for t in range(NT):
                    for k in range(KT):
                        ins = pe.matmul(gbank(s, g)[:, t * D:(t + 1) * D], slots[s].yT[:, k, t * P:(t + 1) * P],
                                        w[:, k, c0:c0 + D], start=(k == 0), stop=(k == KT - 1))
                ins.then_inc(sem("g_written"), 1)

            def scores(i, s, a, p):
                z = slots[s]
                rep = (1, NH // NKV)[a]
                units = order_of(i, s, a) * PAIRS
                if p == 0:
                    pe.wait_ge(sem(f"qst{a}{s}"), 16 * 5 * (i + 1))
                    pe.wait_ge(sem(f"kst{a}{s}"), 16 * 4 * (i + 1))
                if p < 2:
                    wait_met(pe, sem("exp"), units - 1 + p)
                else:
                    pe.wait_ge(sem("max"), units + p - 1)
                for u in range(2):
                    h = 2 * p + u
                    o = bank[2 * (p % 2) + u]
                    pe.matmul(o[:, 0:SC], identb[:], mask_s[:, a], start=True, stop=False)
                    pe.matmul(o[:, 0:QC], z.qst[:, h, 0:P], z.kst[a][:, h // rep, 0:QC],
                              start=False, stop=False)
                    ins = pe.matmul(o[:, QC:SC], z.qst[:, h, P:2 * P], z.kst[a][:, h // rep, :],
                                    start=False, stop=True)
                ins.then_inc(sem("s"), 1)

            def maxima_T(i, s, a):
                z = slots[s]
                g_free(pe, i, s, f"mt{a + 1}")
                pe.wait_ge(sem("nm"), order_of(i, s, a) + 1)
                for t in range(NT):
                    ins = pe.transpose(gbank(s, f"mt{a + 1}")[0:32, t * P:(t + 1) * P],
                                       z.nm[:, t].rearrange("p a h -> p (a h)").bitcast(F32), ident[:])
                ins.then_inc(sem("g_written"), 1)

            def values(i, s, a, p):
                z = slots[s]
                rep = (1, NH // NKV)[a]
                pe.wait_ge(sem("exp"), order_of(i, s, a) * PAIRS + p + 1)
                for u in range(2):
                    h = 2 * p + u
                    w = prob[p % 2][:, u]
                    c = slice(h * (HD + 1), (h + 1) * (HD + 1))
                    pe.matmul(bank[4][:, c], w[:, 0:P], z.v[a][:, 0, h // rep], start=True, stop=True)
                    pe.matmul(bank[5][:, c], w[:, P:2 * P], z.v[a][:, 0, h // rep], start=True, stop=False)
                    ins = pe.matmul(bank[5][:, c], w[:, 2 * P:TC], z.v[a][:, 1, h // rep], start=False, stop=True)
                ins.then_inc(sem("pv"), 1)

            def scores_T(i, s, a, p):
                z = slots[s]
                rep = (1, NH // NKV)[a]
                units = order_of(i, s, a) * PAIRS
                if p == 0:
                    pe.wait_ge(sem(f"mrow{a}{s}"), 16 * 2 * (i + 1))
                if p < 2:
                    pe.wait_ge(sem("max"), units + PAIRS - 1 + p)
                else:
                    pe.wait_ge(sem("exp"), units + p - 1)
                for u in range(2):
                    h = 2 * p + u
                    o = bank[2 * (p % 2) + u]
                    pe.matmul(o[:, 0:TC], identb[:], mask_t[:, a], start=True, stop=False)
                    pe.matmul(o[:, 0:2 * P], z.kst[a][:, h // rep, 2:P + 2], z.qst[:, h],
                              start=False, stop=False)
                    ins = pe.matmul(o[:, 2 * P:TC], z.kst[a][:, h // rep, P + 2:KC], z.qst[:, h, P:2 * P],
                                    start=False, stop=True)
                ins.then_inc(sem("st"), 1)
                if p == 1:
                    wait_met(pe, sem("osum"), order_of(i, s, a) * NT)
                    if a == 1:
                        pe.wait_ge(sem("v2"), i * 2 + s + 1)
                if p >= 1:
                    values(i, s, a, p - 1)

            def project_qkv2(i, s):
                for t, g in enumerate(("qkv2a", "qkv2b")):
                    if t == 0:
                        pe.wait_ge(*read(i, s, "tr_y2"))
                    g_free(pe, i, s, g)
                    for k in range(KT):
                        ins = pe.matmul(gbank(s, g)[:, 0:384], slots[s].yT[:, k, t * P:(t + 1) * P], w_qkv2[:, k],
                                        start=(k == 0), stop=(k == KT - 1))
                    ins.then_inc(sem("g_written"), 1)

            def turned_T(i, s):
                z = slots[s]
                g_free(pe, i, s, "tr_q2")
                g_free(pe, i, s, "tr_k2")
                pe.wait_ge(sem("rope_p"), (i * 2 + s) * 3 + 3)
                pe.wait_ge(sem("rope_v"), (i * 2 + s) * 3 + 3)
                rot = z.rot[:].rearrange("p t h d -> p t (h d)")
                for m in range(2):
                    for t in range(NT):
                        ins = pe.transpose(gbank(s, "tr_q2")[:, m * 2 * P + t * P:m * 2 * P + (t + 1) * P],
                                           rot[:, t, m * P:(m + 1) * P], ident[:])
                ins.then_inc(sem("g_written"), 1)
                for t in range(NT):
                    ins = pe.transpose(gbank(s, "tr_k2")[0:64, t * P:(t + 1) * P], rot[:, t, D:D + 64], ident[:])
                ins.then_inc(sem("g_written"), 1)

            def project_v1(i, s):
                pe.wait_ge(*read(i, s, "tr_y1"))
                project(i, s, "v1", w_qkv1, 2 * D)

            def project_qk1(i, s):
                project_T(i, s, "q1", w_qkv1, 0)
                project_T(i, s, "k1", w_qkv1, D)

            def project_out(i, s, a):
                pe.wait_ge(*read(i, s, f"tr_o{a + 1}"))
                project(i, s, f"out{a + 1}", (w_out1, w_out2)[a], 0)

            def logits(i, s):
                pe.wait_ge(*read(i, s, "tr_x"))
                g_free(pe, i, s, "lgt")
                for t in range(NT):
                    for k in range(KT):
                        ins = pe.matmul(gbank(s, "lgt")[:, t * NE:(t + 1) * NE],
                                        slots[s].yT[:, k, t * P:(t + 1) * P], w_gate[:, k],
                                        start=(k == 0), stop=(k == KT - 1))
                ins.then_inc(sem("g_written"), 1)

            def ranks(i, s):
                z = slots[s]
                g_free(pe, i, s, "rank")
                pe.wait_ge(sem("pick"), i * 2 + s + 1)
                gb = gbank(s, "rank")
                pe.matmul(gb[:, 0:NE], prefix[:, 0], z.pick[:, 0], start=True, stop=True)
                for c in (1, 2):
                    pe.matmul(gb[:, c * NE:(c + 1) * NE], prefix[:, c - 1], z.pick[:, 1], start=True, stop=False)
                    ins = pe.matmul(gb[:, c * NE:(c + 1) * NE], prefix[:, 1], z.pick[:, 0], start=False, stop=True)
                ins.then_inc(sem("g_written"), 1)

            share = {"conv": conv, "tr_y1": lambda i, s: tr(i, s, "tr_y1", slots[s].y, "ln1"),
                     "qk1": project_qk1, "v1": project_v1,
                     "tr_o1": lambda i, s: tr(i, s, "tr_o1", slots[s].tmp, "on0"),
                     "out1": lambda i, s: project_out(i, s, 0),
                     "tr_y2": lambda i, s: tr(i, s, "tr_y2", slots[s].hn, "hn"),
                     "qkv2": project_qkv2, "qk2": turned_T,
                     "tr_o2": lambda i, s: tr(i, s, "tr_o2", slots[s].tmp, "on1"),
                     "out2": lambda i, s: project_out(i, s, 1),
                     "tr_x": lambda i, s: tr(i, s, "tr_x", slots[s].xn, "xn"), "lgt": logits, "rank": ranks}
            for a in range(2):
                share[f"mt{a}"] = lambda i, s, a=a: maxima_T(i, s, a)
                share[f"pv{a}"] = lambda i, s, a=a: values(i, s, a, PAIRS - 1)
                for n in range(PAIRS):
                    share[f"s{n}{a}"] = lambda i, s, a=a, n=n: scores(i, s, a, n)
                    share[f"st{n}{a}"] = lambda i, s, a=a, n=n: scores_T(i, s, a, n)
            go_through(pe, share)

            pe.wait_ge(sem("w13_split"), KT * NE)

            def expert_of(t):
                return pe.value_load(tile_i[0:1, 0, t], min_val=0, max_val=NE - 1)

            def turn_tokens(t, n, buffer_use):
                pe.wait_ge(sem(f"xt{n}"), 16 * buffer_use)
                for k in range(KT):
                    ins = pe.transpose(bank[0][:, k * P:(k + 1) * P], xt[n][:, k * P:(k + 1) * P], ident[:])
                ins.then_inc(sem("tr_e"), 1)

            def up(t, n):
                e = expert_of(tile(t))
                pe.wait_ge(sem("xT"), t + 1)
                for half in range(2):
                    for k in range(KT):
                        for m, (part, w) in enumerate(((0, w13h), (0, w13l), (1, w13h))):
                            ins = pe.matmul(bank[2 + 2 * n + half][:], xT[n][:, part, k * P:(k + 1) * P],
                                            w[:, k, bass.ds(e, 1), half * FFN:(half + 1) * FFN],
                                            start=(k == 0 and m == 0), stop=(k == KT - 1 and m == 2))
                ins.then_inc(sem("up"), 1)

            def turn_hidden(t, n):
                pe.wait_ge(sem("gu"), t + 1)
                for f in range(FT):
                    ins = pe.transpose(bank[6][:, f * P:(f + 1) * P], gu[n][:, f * P:(f + 1) * P], ident[:])
                ins.then_inc(sem("tr_g"), 1)

            def down(t, n):
                e = expert_of(tile(t))
                pe.wait_ge(sem("guT"), t + 1)
                for f in range(FT):
                    ins = pe.matmul(bank[(1, 7)[n]][:, 0:D], guT[n][:, f], w2s[:, f, bass.ds(e, 1), :],
                                    start=(f == 0), stop=(f == FT - 1))
                ins.then_inc(sem("down"), 1)

            def expert_step(t, n, buffer_use):
                turn_hidden(t - 1, 1 - n)
                up(t, n)
                if buffer_use is not None:
                    turn_tokens(t + 1, 1 - n, buffer_use)
                down(t - 1, 1 - n)

            turn_tokens(0, 0, 1)
            up(0, 0)
            turn_tokens(1, 1, 1)
            pe.wait_ge(sem("w2"), 16)
            expert_step(1, 1, 2)
            expert_step(2, 0, 2)
            with pe.Fori(0, EPAIRS) as j:
                expert_step(j * 2 + 3, 1, j + 3)
                expert_step(j * 2 + 4, 0, j + 3)
            expert_step(MT - 1, 1, None)
            turn_hidden(MT - 1, 1)
            down(MT - 1, 1)

        @block.vector
        def _(dve):
            dve.wait_ge(sem("const"), 16 * 14)
            chain = [0]

            def link(ins):
                chain[0] += 1
                ins.then_inc(sem("dve_chain"), 1)
                dve.wait_ge(sem("dve_chain"), chain[0])

            dve.tensor_copy(mask_s[:].rearrange("p a c -> p (a c)"), stage[:, 0:2 * SC]).then_inc(sem("mask_s_cast"), 1)
            dve.tensor_copy(identb[:], ident[:]).then_inc(sem("masks"), 1)
            dve.wait_ge(sem("stage2"), 16)
            dve.tensor_copy(mask_t[:].rearrange("p a c -> p (a c)"), stage[:, 0:2 * TC]).then_inc(sem("mask_t_cast"), 1)
            dve.wait_ge(sem("stage3"), 16)
            dve.tensor_copy(prefix[:].rearrange("p a c -> p (a c)"), stage[:, 0:2 * P]).then_inc(sem("masks"), 2)
            for f in range(2):
                for dx in range(3):
                    link(dve.tensor_scalar(band[:, f, dx], shift[:, 0], taps[:, f, 0, dx:dx + 1], None, ALU.mult))
                    for dy in range(1, 3):
                        link(dve.scalar_tensor_tensor(out=band[:, f, dx], in0=shift[:, dy],
                                                      scalar=taps[:, f, dy, dx:dx + 1], in1=band[:, f, dx],
                                                      op0=ALU.mult, op1=ALU.add))
            for k in range(KT):
                link(dve.tensor_scalar(w_qkv2[:, k], w_qkv2[:, k], lnw[:, 0, k:k + 1], None, ALU.mult))
                link(dve.tensor_scalar(w_gate[:, k], w_gate[:, k], lnw[:, 1, k:k + 1], None, ALU.mult))
            dve.tensor_scalar(Z.va[:, 1:2], small[:, 0:1], 0.0, None, ALU.mult).then_inc(sem("bands"), 1)
            dve.tensor_scalar(Z.vb[:, 1:2], small[:, 0:1], 0.0, None, ALU.mult).then_inc(sem("scaled_w"), 1)

            c = sem("cls")
            dve.wait_ge(sem("cleared"), 20)
            dve.wait_ge(sem("mask_t_cast"), 1)
            dve.tensor_copy(Z.rr[:, 0:1], small[:, 41:42]).then_inc(c, 1)
            dve.tensor_copy(Z.rr[:, 1:2], small[:, 41:42]).then_inc(c, 1)

            def d(name, f, *args, **kw):
                dve.wait_ge(c, CLS.index(name))
                f(*args, **kw).then_inc(c, 1)

            def cstats(x, n):
                d("bn" + n, dve.bn_stats, Z.bn[:, 0], x)
                d("aggr" + n, dve.bn_aggr, Z.st[:, 0], Z.bn[:, 0])

            cstats(Z.h0[:, 0], "")
            d("var", dve.tensor_scalar, Z.va[:, 0:1], Z.st[:, 0, 1:2], EPS, None, ALU.add)
            d("ln", dve.tensor_scalar, Z.y[:, 0], Z.h0[:, 0], Z.st[:, 0, 0:1], Z.rstd[:, 0:1], ALU.subtract, ALU.mult)
            kps = bank[4][:, 0:2 * P].rearrange("p (m q) -> p m q", m=2)[:, :, 0:2]
            d("kh", dve.tensor_copy, Z.khl[:, 0, :, 0:2], kps)
            d("kl", dve.tensor_tensor, Z.khl[:, 1, :, 0:2], kps, Z.khl[:, 0, :, 0:2].bitcast(F32), ALU.subtract)
            vps = bank[7][:, 0:D].rearrange("p (h d) -> p h d", h=NH)
            d("vcopy", dve.tensor_copy, vc[0][:, :, 0:HD], vps)
            d("kdma", dve.tensor_copy, Z.tmp[:, 0].rearrange("p (h d) -> p h d", h=NH), vc[0][:, :, 0:HD])
            d("res", dve.tensor_tensor, Z.h0[:, 0], Z.h0[:, 0], bank[7][:, 0:D], ALU.add)
            cstats(Z.h0[:, 0], "2")
            d("var2", dve.tensor_scalar, Z.va[:, 0:1], Z.st[:, 0, 1:2], EPS, None, ALU.add)
            d("va2", dve.tensor_tensor, Z.vb[:, 0:1], Z.rstd[:, 0:1], Z.rstd[:, 0:1], ALU.mult)
            d("vb2", dve.tensor_scalar, Z.vb[:, 0:1], Z.vb[:, 0:1], Z.st[:, 0, 1:2], EPS, ALU.mult, ALU.add)
            d("y2", dve.tensor_scalar, Z.y[:, 0], Z.h0[:, 0], Z.st[:, 0, 0:1], Z.rstd[:, 0:1], ALU.subtract, ALU.mult)
            d("hn2", dve.tensor_scalar, Z.hn[:, 0], Z.y[:, 0], Z.rr[:, 0:1], None, ALU.mult)
            kps2 = bank[4][0:64, 0:2]
            dve.wait_ge(sem("kcls_out"), 16)
            d("kh2", dve.tensor_copy, Z.khl[0:64, 0, 0, 0:2], kps2)
            d("kl2", dve.tensor_tensor, Z.khl[0:64, 1, 0, 0:2], kps2, Z.khl[0:64, 0, 0, 0:2].bitcast(F32), ALU.subtract)
            d("vcopy2", dve.tensor_copy, vc[1][:, :, 0:HD].rearrange("p (g r) d -> p g r d", g=NKV),
              Z.qkv[:, 0, 20:24, :].unsqueeze(2).broadcast_to([P, NKV, NH // NKV, HD]))
            d("kdma2", dve.tensor_copy, Z.tmp[:, 0].rearrange("p (h d) -> p h d", h=NH), vc[1][:, :, 0:HD])
            d("x2", dve.tensor_tensor, Z.y[:, 0], Z.y[:, 0], bank[7][:, 0:D], ALU.add)
            d("res2", dve.tensor_tensor, cls_res[:], Z.y[:, 0], Z.h0[:, 0], ALU.add)
            cstats(Z.y[:, 0], "3")
            d("sq3", dve.tensor_tensor, Z.vb[:, 0:1], Z.st[:, 0, 0:1], Z.st[:, 0, 0:1], ALU.mult)
            d("var3", dve.tensor_scalar, Z.va[:, 0:1], Z.vb[:, 0:1], Z.st[:, 0, 1:2], EPS, ALU.add, ALU.add)
            d("xn3", dve.tensor_scalar, Z.xn[:, 0], Z.y[:, 0], Z.rr[:, 0:1], None, ALU.mult)
            ro = route[:, RT - 1]
            d("lgtc", dve.tensor_copy, Z.lg[:, 0], bank[7][:, 0:NE])
            d("max", dve.max, Z.top[:, 0], Z.lg[:, 0])
            d("midx", dve.max_index, Z.idx[:, 0], Z.top[:, 0], Z.lg[:, 0])
            d("midf", dve.tensor_copy, ro[:, 0:2], Z.idx[:, 0, 0:2])
            d("dif", dve.tensor_tensor, Z.ew[:, 0, 0:1], Z.top[:, 0, 1:2], Z.top[:, 0, 0:1], ALU.subtract)
            d("den", dve.tensor_scalar, Z.ew[:, 0, 1:2], Z.ew[:, 0, 0:1], 1.0, None, ALU.add)
            d("w0", dve.reciprocal, ro[:, 4:5], Z.ew[:, 0, 1:2])
            d("w1", dve.tensor_tensor, ro[:, 5:6], Z.ew[:, 0, 0:1], ro[:, 4:5], ALU.mult)
            for k in range(2):
                d(f"oh{k}", dve.tensor_scalar, Z.oh[:, 0, k], small[:, 0:8], ro[:, k:k + 1], None, ALU.is_equal)
            d("cnt", dve.tensor_tensor, counts[:], Z.oh[:, 0, 0], Z.oh[:, 0, 1], ALU.add)
            d("rank0", dve.memset, ro[:, 2:4], 0.0)
            d("pose", dve.tensor_scalar, Z.posf[:, 0], ro[:, 0:2], float(REGION), None, ALU.mult)
            d("posm", dve.tensor_scalar, Z.posf[:, 0], Z.posf[:, 0], small[:, 42:43], None, ALU.mult)
            d("posd", dve.tensor_tensor, Z.posf[:, 0], Z.posf[:, 0], small[:, 43:45], ALU.add)
            d("posi", dve.tensor_copy, Z.pos[:, 0], Z.posf[:, 0])
            for k in range(2):
                dve.wait_ge(sem(f"scat{k}"), 16)
            dve.wait_ge(c, CLS.index("scat"))
            dve.tensor_copy(Z.va[:, 0:1], small[:, 0:1]).then_inc(c, 1)
            dve.wait_ge(sem("kcls"), 16 * 16)

            def made(s, name):
                at[0].place[s, name] = len(at[0].place) + 1
                return sem("vector_own"), 1

            def own(i, s, name):
                return sem("vector_own"), turn(BODY_OWN) + at[0].own_before + at[0].place[s, name]

            def gray(i, s):
                z = slots[s]
                dve.wait_ge(sem(f"xin{s}"), 32 * (i + 1))
                g = z.gray[:, :, 1:HW + 1]
                wait_met(dve, sem(f"halo{s}"), 96 * i)
                dve.tensor_scalar(g, z.xin[:, :, 0], GRAY[0], None, ALU.mult).then_inc(*made(s, "g1"))
                dve.wait_ge(*own(i, s, "g1"))
                dve.scalar_tensor_tensor(out=g, in0=z.xin[:, :, 1], scalar=GRAY[1], in1=g, op0=ALU.mult,
                                         op1=ALU.add).then_inc(*made(s, "g2"))
                dve.wait_ge(*own(i, s, "g2"))
                dve.scalar_tensor_tensor(out=g, in0=z.xin[:, :, 2], scalar=GRAY[2], in1=g, op0=ALU.mult,
                                         op1=ALU.add).then_inc(sem("gray"), 1)

            def stats(i, s, n, x, ready):
                z = slots[s]
                dve.wait_ge(*ready)
                for t in range(NT):
                    ins = dve.bn_stats(z.bn[:, t], x[:, t])
                ins.then_inc(*made(s, f"bn{n}"))
                dve.wait_ge(*own(i, s, f"bn{n}"))
                dve.memset(idle[:, 0:1], 0.0)
                for t in range(NT):
                    ins = dve.bn_aggr(z.st[:, t], z.bn[:, t])
                ins.then_inc(*made(s, f"st_{n}"))
                dve.wait_ge(*own(i, s, f"st_{n}"))

            def lowpart(i, s, a, g, key, dst, src, hi, scale):
                dve.wait_ge(sem(f"{key}hi{a}"), i * 2 + s + 1)
                dve.scalar_tensor_tensor(out=dst, in0=src, scalar=scale, in1=hi.bitcast(F32), op0=ALU.mult,
                                         op1=ALU.subtract).then_inc(read_sem(s, g), 1)

            def full(s, g):
                return gbank(s, g)[:].rearrange("p (k q) -> p k q", k=2)

            def maxima(i, s, a, p):
                z = slots[s]
                units = order_of(i, s, a) * PAIRS
                dve.wait_ge(sem("s"), units + p + 1)
                o = unit[p % 2]
                heads = slice(2 * p, 2 * p + 2)
                dve.tensor_copy(z.scls[:, :, heads].rearrange("p t h -> p h t"), o[:, :, 0:QC + 1:QC])
                dve.tensor_reduce(z.mx[:, 0, heads], o[:, :, 0:QC], AX.X, ALU.max)
                dve.tensor_reduce(z.mx[:, 1, heads], o[:, :, QC:SC], AX.X, ALU.max).then_inc(sem("max"), 1)
                if p == PAIRS - 1:
                    dve.wait_ge(sem("max"), units + PAIRS)
                    dve.tensor_scalar(z.nm[:, :, 0], z.mx[:], -1.0, None, ALU.mult).then_inc(*made(s, f"nmh{a}"))
                    dve.tensor_tensor(z.pcls[:], z.scls[:], z.mx[:], ALU.subtract).then_inc(sem("dcls"), 1)
                    dve.wait_ge(*own(i, s, f"nmh{a}"))
                    dve.scalar_tensor_tensor(out=z.nm[:, :, 1], in0=z.mx[:], scalar=-1.0,
                                             in1=z.nm[:, :, 0].bitcast(F32), op0=ALU.mult, op1=ALU.subtract)\
                        .then_inc(sem("nm"), 1)

            def outputs(i, s, a):
                z = slots[s]
                nth = order_of(i, s, a)
                dve.wait_ge(sem("pv"), (nth + 1) * PAIRS)
                dve.wait_ge(sem("ocls"), (nth + 1) * NT)
                for t in range(NT):
                    dve.tensor_tensor(z.osum[:, t].rearrange("p h d -> p (h d)"), bank[4 + t][:, 0:NH * (HD + 1)],
                                      z.ocls[:, t].rearrange("p h d -> p (h d)"), ALU.add).then_inc(sem("osum"), 1)
                dve.wait_ge(sem("osum"), (nth + 1) * NT)
                dve.reciprocal(z.rden[:], z.osum[:, :, :, HD]).then_inc(*made(s, f"rden{a}"))
                dve.wait_ge(*own(i, s, f"rden{a}"))
                dve.tensor_tensor(z.tmp[:].rearrange("p t (h d) -> p t h d", h=NH), z.osum[:, :, :, 0:HD],
                                  z.rden[:].unsqueeze(3).broadcast_to([P, NT, NH, HD]), ALU.mult)\
                    .then_inc(sem(f"on{a}"), 1)

            def sum1(i, s):
                z = slots[s]
                dve.wait_ge(*read(i, s, "conv0"))
                dve.wait_ge(*read(i, s, "conv1"))
                dve.tensor_tensor(z.h0[:], z.h0[:], z.tmp[:], ALU.add).then_inc(sem("h0"), 1)
                stats(i, s, 1, z.h0, (sem("h0"), i * 2 + s + 1))
                dve.tensor_scalar(z.va[:], z.st[:, :, 1], EPS, None, ALU.add).then_inc(sem("va1"), 1)

            def norm1(i, s):
                z = slots[s]
                dve.wait_ge(sem("rstd1"), i * 2 + s + 1)
                for t in range(NT):
                    ins = dve.tensor_scalar(z.y[:, t], z.h0[:, t], z.st[:, t, 0:1], z.rstd[:, t:t + 1],
                                            ALU.subtract, ALU.mult)
                ins.then_inc(sem("ln1"), 1)

            def low1(i, s):
                z = slots[s]
                lowpart(i, s, 0, "q1", "q", z.qhl[:, 1], full(s, "q1"), z.qhl[:, 0], 0.25)
                lowpart(i, s, 0, "k1", "k", z.khl[:, 1], full(s, "k1"), z.khl[:, 0], 1.0)

            def sum2(i, s):
                z = slots[s]
                dve.wait_ge(*written(i, s, "out1"))
                dve.tensor_tensor(z.h0[:], z.h0[:], full(s, "out1"), ALU.add).then_inc(read_sem(s, "out1"), 1)
                stats(i, s, 2, z.h0, read(i, s, "out1"))
                dve.tensor_scalar(z.va[:], z.st[:, :, 1], EPS, None, ALU.add).then_inc(sem("va2"), 1)

            def norm2(i, s):
                z = slots[s]
                dve.wait_ge(sem("rstd2"), i * 2 + s + 1)
                dve.tensor_tensor(z.vb[:], z.rstd[:], z.rstd[:], ALU.mult).then_inc(*made(s, "vr"))
                for t in range(NT):
                    ins = dve.tensor_scalar(z.y[:, t], z.h0[:, t], z.st[:, t, 0:1], z.rstd[:, t:t + 1],
                                            ALU.subtract, ALU.mult)
                ins.then_inc(*made(s, "y2"))
                dve.wait_ge(*own(i, s, "vr"))
                dve.tensor_tensor(z.vb[:], z.vb[:], z.st[:, :, 1], ALU.mult).then_inc(*made(s, "vs"))
                dve.wait_ge(*own(i, s, "vs"))
                dve.tensor_scalar(z.vb[:], z.vb[:], EPS, None, ALU.add).then_inc(sem("vb2"), 1)

            def norm3(i, s):
                z = slots[s]
                dve.wait_ge(*own(i, s, "y2"))
                dve.wait_ge(sem("rr2"), i * 2 + s + 1)
                dve.wait_ge(sem(f"scat{s}"), 64 * i + 16)
                for t in range(NT):
                    ins = dve.tensor_scalar(z.hn[:, t], z.y[:, t], z.rr[:, t:t + 1], None, ALU.mult)
                ins.then_inc(sem("hn"), 1)

            def rope_first(i, s):
                z = slots[s]
                dve.wait_ge(*read(i, s, "qkv2b"))
                x1, x2 = z.qkv[:, :, 0:20, 0:8], z.qkv[:, :, 0:20, 8:16]
                co = rope[:, 0].unsqueeze(2).broadcast_to([P, NT, 20, 8])
                si = rope[:, 1].unsqueeze(2).broadcast_to([P, NT, 20, 8])
                r0 = z.ra[:, 0].rearrange("p (t h d) -> p t h d", t=NT, h=20)
                r1 = z.ra[:, 1].rearrange("p (t h d) -> p t h d", t=NT, h=20)
                dve.tensor_tensor(r0, x1, co, ALU.mult).then_inc(sem("rope_v"), 1)
                dve.tensor_tensor(r1, x2, si, ALU.mult).then_inc(sem("rope_v"), 1)
                dve.wait_ge(sem("rope_v"), (i * 2 + s) * 3 + 2)
                dve.tensor_tensor(z.rot[:, :, :, 0:8], r0, r1, ALU.subtract).then_inc(sem("rope_v"), 1)

            def low2(i, s):
                z = slots[s]
                lowpart(i, s, 1, "tr_q2", "q", z.qhl[:, 1], full(s, "tr_q2"), z.qhl[:, 0], 0.25)
                lowpart(i, s, 1, "tr_k2", "k", z.khl[0:64, 1, 0], gbank(s, "tr_k2")[0:64, 0:256],
                        z.khl[0:64, 0, 0], 1.0)

            def sum3(i, s):
                z = slots[s]
                dve.wait_ge(*written(i, s, "out2"))
                dve.tensor_tensor(z.y[:], z.y[:], full(s, "out2"), ALU.add).then_inc(read_sem(s, "out2"), 1)
                stats(i, s, 3, z.y, read(i, s, "out2"))
                dve.tensor_tensor(z.vb[:], z.st[:, :, 0], z.st[:, :, 0], ALU.mult).then_inc(*made(s, "ms"))
                dve.wait_ge(*own(i, s, "ms"))
                dve.scalar_tensor_tensor(out=z.va[:], in0=z.vb[:], scalar=EPS, in1=z.st[:, :, 1], op0=ALU.add,
                                         op1=ALU.add).then_inc(sem("va3"), 1)
                dve.wait_ge(sem(f"res_saved{s}"), 16 * i + 1)
                dve.tensor_tensor(z.res[:], z.y[:], z.h0[:], ALU.add).then_inc(sem("res"), 1)

            def norm4(i, s):
                z = slots[s]
                dve.wait_ge(sem("rr3"), i * 2 + s + 1)
                for t in range(NT):
                    ins = dve.tensor_scalar(z.xn[:, t], z.y[:, t], z.rr[:, t:t + 1], None, ALU.mult)
                ins.then_inc(sem("xn"), 1)

            def choose(i, s):
                z = slots[s]
                dve.wait_ge(*written(i, s, "lgt"))
                dve.tensor_copy(z.lg[:], gbank(s, "lgt")[:, 0:NT * NE].rearrange("p (t e) -> p t e", t=NT))\
                    .then_inc(read_sem(s, "lgt"), 1)
                dve.wait_ge(*read(i, s, "lgt"))
                dve.memset(idle[:, 0:1], 0.0)
                for t in range(NT):
                    ins = dve.max(z.top[:, t], z.lg[:, t])
                ins.then_inc(*made(s, "top"))
                dve.wait_ge(*own(i, s, "top"))
                dve.tensor_tensor(z.ew[:, :, 0], z.top[:, :, 1], z.top[:, :, 0], ALU.subtract)\
                    .then_inc(sem("dtop"), 1)
                for t in range(NT):
                    ins = dve.max_index(z.idx[:, t], z.top[:, t], z.lg[:, t])
                ins.then_inc(*made(s, "idx"))
                dve.wait_ge(*own(i, s, "idx"))
                dve.tensor_copy(z.ro[:, :, 0:2], z.idx[:, :, 0:2]).then_inc(*made(s, "ro_e"))
                dve.wait_ge(*own(i, s, "ro_e"))
                for t in range(NT):
                    for k in range(2):
                        ins = dve.tensor_scalar(z.oh[:, t, k], small[:, 0:8], z.ro[:, t, k:k + 1], None, ALU.is_equal)
                ins.then_inc(*made(s, "oh"))
                dve.wait_ge(*own(i, s, "oh"))
                dve.tensor_tensor(z.pick[:], z.oh[:, :, 0], z.oh[:, :, 1], ALU.add).then_inc(sem("pick"), 1)

            def rank(i, s):
                z = slots[s]
                dve.wait_ge(sem("etop"), i * 2 + s + 1)
                dve.tensor_scalar(z.ew[:, :, 1], z.ew[:, :, 0], 1.0, None, ALU.add).then_inc(*made(s, "wd"))
                dve.wait_ge(*own(i, s, "wd"))
                dve.reciprocal(z.ro[:, :, 4], z.ew[:, :, 1]).then_inc(*made(s, "w0"))
                dve.wait_ge(*own(i, s, "w0"))
                dve.tensor_tensor(z.ro[:, :, 5], z.ew[:, :, 0], z.ro[:, :, 4], ALU.mult).then_inc(*made(s, "w1"))
                dve.wait_ge(*written(i, s, "rank"))
                gb = gbank(s, "rank")
                dve.tensor_tensor(z.rk[:], gb[:, 0:2 * NE].rearrange("p (t e) -> p t e", t=NT),
                                  counts[:].unsqueeze(1).broadcast_to([P, NT, NE]), ALU.add)\
                    .then_inc(*made(s, "rk"))
                dve.wait_ge(*own(i, s, "rk"))
                dve.tensor_tensor(counts[:], counts[:], gb[:, 2 * NE:3 * NE], ALU.add).then_inc(read_sem(s, "rank"), 1)
                dve.tensor_tensor(z.rsel[:], z.oh[:], z.rk[:].unsqueeze(2).broadcast_to([P, NT, 2, NE]), ALU.mult)\
                    .then_inc(*made(s, "rsel"))
                dve.wait_ge(*own(i, s, "rsel"))
                dve.tensor_reduce(z.ro[:, :, 2:4], z.rsel[:], AX.X, ALU.add).then_inc(*made(s, "ro_r"))
                dve.wait_ge(*own(i, s, "ro_r"))
                dve.wait_ge(*read(i, s, "rank"))
                dve.wait_ge(*own(i, s, "w1"))
                dve.scalar_tensor_tensor(out=z.posf[:], in0=z.ro[:, :, 0:2], scalar=float(REGION), in1=z.ro[:, :, 2:4],
                                         op0=ALU.mult, op1=ALU.add).then_inc(*made(s, "posf"))
                dve.tensor_copy(route[:, bass.ds((i * 2 + s) * NT, NT), :], z.ro[:]).then_inc(sem("routed"), 1)
                dve.wait_ge(*own(i, s, "posf"))
                dve.tensor_copy(z.pos[:], z.posf[:]).then_inc(sem("pos"), 1)

            share = {"gray": gray, "sum1": sum1, "norm1": norm1, "qk1": low1, "out1": sum2, "norm2": norm2,
                     "hn": norm3, "rope": rope_first, "qk2": low2, "out2": sum3, "xn": norm4, "lgt": choose,
                     "rank": rank}
            for a in range(2):
                share[f"o{a + 1}"] = lambda i, s, a=a: outputs(i, s, a)
                for n in range(PAIRS):
                    share[f"s{n}{a}"] = lambda i, s, a=a, n=n: maxima(i, s, a, n)
            go_through(dve, share)
            assert len(first.place) == FIRST_OWN and len(body.place) == BODY_OWN, (len(first.place), len(body.place))

            for s in range(2):
                dve.wait_ge(sem("routed"), B)
                dve.wait_ge(sem(f"scat{s}"), 64 * ITERS + 16)
                dve.wait_ge(sem(f"res_saved{s}"), 16 * ITERS + 1)
            link(dve.tensor_tensor(gt[:], counts[:].unsqueeze(2).broadcast_to([P, NE, 33]),
                                   small[:, 8:41].unsqueeze(1).broadcast_to([P, NE, 33]), ALU.is_gt))
            link(dve.tensor_reduce(nt[:], gt[:], AX.X, ALU.add))
            link(dve.memset(start[:], 0.0))
            link(dve.memset(zrow[:], 0.0))
            for e in range(1, NE):
                link(dve.tensor_tensor(start[:, e:e + 1], start[:, e - 1:e], nt[:, e - 1:e], ALU.add))
            link(dve.tensor_tensor(zposf[:, 0], counts[:], small[:, 45:53], ALU.add))
            link(dve.tensor_scalar(zposf[:, 0], zposf[:, 0], small[:, 41:42], None, ALU.add))
            link(dve.tensor_scalar(zposf[:, 1], zposf[:, 0], float(P), None, ALU.add))
            dve.tensor_copy(zpos[:], zposf[:]).then_inc(sem("zpos"), 1)
            link(dve.tensor_tensor(over[:], small[:, 64:64 + MT].unsqueeze(1).broadcast_to([P, NE, MT]),
                                   start[:].unsqueeze(2).broadcast_to([P, NE, MT]), ALU.is_ge))
            link(dve.tensor_reduce(tile_e[:], over[:, 1:NE].rearrange("p e j -> p j e"), AX.X, ALU.add))
            link(dve.tensor_tensor(over[:, 1:NE], over[:, 1:NE],
                                   nt[:, 0:NE - 1].unsqueeze(2).broadcast_to([P, NE - 1, MT]), ALU.mult))
            link(dve.tensor_reduce(tile_s[:], over[:, 1:NE].rearrange("p e j -> p j e"), AX.X, ALU.add))
            link(dve.tensor_tensor(tile_l[:], small[:, 64:64 + MT], tile_s[:], ALU.subtract))
            link(dve.tensor_scalar(cap[:], tile_e[:], -1000.0, 1000.0 * (NE - 1), ALU.mult, ALU.add))
            link(dve.tensor_scalar(cap[:], cap[:], nt[:, NE - 1:NE], None, ALU.add))
            link(dve.tensor_tensor(tile_l[:], tile_l[:], cap[:], ALU.min))
            link(dve.tensor_scalar(tile_l[:], tile_l[:], float(P), None, ALU.mult))
            link(dve.scalar_tensor_tensor(out=tile_l[:], in0=tile_e[:], scalar=float(REGION), in1=tile_l[:],
                                          op0=ALU.mult, op1=ALU.add))
            link(dve.tensor_copy(tile_i[:, 0], tile_e[:]))
            dve.tensor_copy(tile_i[:, 1], tile_l[:]).then_inc(sem("tile_i"), 1)
            link(dve.tensor_tensor(eqs[:].rearrange("p (t k) e -> p t k e", k=2),
                                   route[:, :, 0:2].unsqueeze(3).broadcast_to([P, RT, 2, NE]),
                                   small[:, 0:8].unsqueeze(1).unsqueeze(1).broadcast_to([P, RT, 2, NE]), ALU.is_equal))
            link(dve.tensor_tensor(eqs[:], eqs[:], start[:].unsqueeze(1).broadcast_to([P, RT * 2, NE]), ALU.mult))
            link(dve.tensor_reduce(yposf[:].rearrange("p t k -> p (t k)"), eqs[:], AX.X, ALU.add))
            link(dve.scalar_tensor_tensor(out=yposf[:], in0=yposf[:], scalar=float(P), in1=route[:, :, 2:4],
                                          op0=ALU.mult, op1=ALU.add))
            link(dve.tensor_copy(ypos[:], yposf[:]))
            dve.wait_ge(sem("lnm"), 16)
            for e in range(NE):
                for k in range(KT):
                    dve.wait_ge(sem("w13_high"), KT * e + k + 1)
                    dve.scalar_tensor_tensor(out=w13l[:, k, e], in0=w13l[:, k, e].bitcast(F32),
                                             scalar=lnm[:, k:k + 1], in1=w13h[:, k, e].bitcast(F32), op0=ALU.mult,
                                             op1=ALU.subtract).then_inc(sem("w13_split"), 1)

            def tokens_low(t, n):
                dve.wait_ge(sem("xT_high"), t + 1)
                dve.tensor_tensor(xT[n][:, 1], bank[0][:, 0:2 * P], xT[n][:, 0].bitcast(F32), ALU.subtract)\
                    .then_inc(sem("xT"), 1)

            def hidden(t, n):
                dve.wait_ge(sem("silu"), t + 1)
                dve.tensor_tensor(gu[n][:], sg[n][:], bank[3 + 2 * n][:], ALU.mult).then_inc(sem("gu"), 1)

            def expert_out(t, n, stored=None):
                dve.wait_ge(sem("down"), t + 1)
                if stored is not None:
                    dve.wait_ge(sem(f"ys{n}"), 16 * stored)
                dve.tensor_copy(yo[n][:], bank[(1, 7)[n]][:, 0:D]).then_inc(sem("yo"), 1)

            tokens_low(0, 0)
            hidden(0, 0)
            tokens_low(1, 1)
            hidden(1, 1)
            tokens_low(2, 0)
            expert_out(0, 0)
            hidden(2, 0)
            tokens_low(3, 1)
            expert_out(1, 1)
            with dve.Fori(0, EPAIRS) as j:
                hidden(j * 2 + 3, 1)
                tokens_low(j * 2 + 4, 0)
                expert_out(j * 2 + 2, 0, j + 1)
                hidden(j * 2 + 4, 0)
                tokens_low(j * 2 + 5, 1)
                expert_out(j * 2 + 3, 1, j + 1)
            hidden(MT - 1, 1)
            expert_out(MT - 2, 0, EPAIRS + 1)
            expert_out(MT - 1, 1, EPAIRS + 1)

            def combine(s, t, dst, res, tag, count):
                dve.scalar_tensor_tensor(out=dst, in0=fy[s][:, t, 0], scalar=fw[s][:, t, 0:1], in1=res,
                                         op0=ALU.mult, op1=ALU.add).then_inc(sem(tag), 1)
                dve.wait_ge(sem(tag), count)
                return dve.scalar_tensor_tensor(out=dst, in0=fy[s][:, t, 1], scalar=fw[s][:, t, 1:2], in1=dst,
                                                op0=ALU.mult, op1=ALU.add)

            with dve.Fori(0, ITERS) as i:
                for s in range(2):
                    dve.wait_ge(sem(f"fo{s}"), i + 1)
                    dve.tensor_copy(fidx[s][:], ypos[:, bass.ds((i * 2 + s) * NT, NT), :]).then_inc(sem(f"fidx{s}"), 1)
                    dve.tensor_copy(fw[s][:], route[:, bass.ds((i * 2 + s) * NT, NT), 4:6]).then_inc(sem(f"fw{s}"), 1)
                for s in range(2):
                    dve.wait_ge(sem(f"fw{s}"), i + 1)
                    dve.wait_ge(sem(f"fy{s}"), 64 * (i + 1))
                    dve.wait_ge(sem(f"fr{s}"), 16 * (i + 1))
                    dve.wait_ge(sem(f"stored{s}"), 32 * i + 1)
                    for t in range(NT):
                        ins = combine(s, t, fo[s][:, t], fr[s][:, t], f"half{s}", i * 2 + t + 1)
                    ins.then_inc(sem(f"fo{s}"), 1)
            dve.tensor_copy(fidx[0][:, 0], ypos[0:P, RT - 1]).then_inc(sem("cls_fi"), 1)
            dve.tensor_copy(fw[0][:, 0], route[:, RT - 1, 4:6]).then_inc(sem("cls_fw"), 1)
            dve.wait_ge(sem("cls_fi"), 1)
            dve.wait_ge(sem("cls_fw"), 1)
            dve.tensor_copy(fw[1][:, 0], route[:, RT - 1, 4:6]).then_inc(sem("cls_fidx"), 1)
            dve.wait_ge(sem("cls_fy"), 32)
            dve.wait_ge(sem("stored0"), 32 * ITERS + 1)
            combine(0, 0, fo[0][:, 0], cls_res[:], "cls_half", 1).then_inc(sem("cls_out"), 1)


def kernel(**inputs):
    import concourse.bacc as _bacc
    from concourse import mybir as _mybir
    from concourse.bass_utils import run_bass_kernel_spmd as _run

    g = {k: np.asarray(v) for k, v in inputs.items()}

    def rows(a, k):
        return np.ascontiguousarray(a.reshape(k, P, -1).transpose(1, 0, 2))

    arrays = {
        "x": g["x"], "cls_tok": g["cls_tok"], "scharr": g["L0_tok_scharr"],
        "wqkv1": rows(g["L0_attn_W_qkv"], KT), "wout1": rows(g["L0_attn_W_out"], KT),
        "ln1": np.ascontiguousarray(g["L0_ffn_ln1_w"].reshape(KT, P).T),
        "ln2": np.ascontiguousarray(g["L0_ffn_ln2_w"].reshape(KT, P).T),
        "wqkv2": rows(g["L0_ffn_wqkv"].T, KT), "wo2": rows(g["L0_ffn_wo"].T, KT),
        "gate": rows(g["L0_ffn_gate_w"].T, KT),
        "w13": np.ascontiguousarray(g["L0_ffn_w13"].transpose(2, 0, 1).reshape(KT, P, NE, 2 * FFN).transpose(1, 0, 2, 3)),
        "w2": np.ascontiguousarray(g["L0_ffn_w2"].transpose(2, 0, 1).reshape(FT, P, NE, D).transpose(1, 0, 2, 3)),
    }
    arrays.update(constants())
    nc = _bacc.Bacc("TRN2", target_bir_lowering=False, num_devices=1)
    in_map, args = {}, []
    for name, a in arrays.items():
        a = np.ascontiguousarray(a)
        in_map[f"in_{name}"] = a
        args.append(nc.dram_tensor(f"in_{name}", a.shape, _mybir.dt.from_np(a.dtype), kind="ExternalInput").ap())
    args.append(nc.dram_tensor("out_0", (B, HW + 1, D), _mybir.dt.float32, kind="ExternalOutput").ap())
    vit_tower(nc, *args)
    r = _run(nc, [in_map], core_ids=[0])
    return r.results[0]["out_0"]
```
